# Optimizing a Trainium2 kernel written in Bass

```python
import numpy as np
import jax
import jax.numpy as jnp

def _softmax(x, axis=-1):
    return jax.nn.softmax(x, axis=axis)

def _gelu(x):
    return jax.nn.gelu(x, approximate=True)

def _silu(x):
    return jax.nn.silu(x)

def _sigmoid(x):
    return jax.nn.sigmoid(x)

def _layernorm(x, axis=-1, eps=1e-05):
    m = jnp.mean(x, axis=axis, keepdims=True)
    v = jnp.var(x, axis=axis, keepdims=True)
    return (x - m) / jnp.sqrt(v + eps)

def _scatter_add(tgt, idx, src, axis=0):
    return tgt.at[idx].add(src)

def _segment_sum(src, seg, n):
    return jax.ops.segment_sum(src, seg, n)
kernel_name = 'mk_early_fusion_d1_tok_img512_r4_da2184'

def setup_inputs(seed: int=0):
    np.random.seed(seed)
    _w = jnp.asarray

    def _rec_inputs():
        import jax
        import jax.numpy as jnp
        _rk = jax.random.key(seed)
        x = -0.000147625 + 0.999875 * jax.random.normal(jax.random.fold_in(_rk, 1), (16, 3, 224, 224), jnp.float32)
        txt = 0.00355565 + 0.408319 * jax.random.normal(jax.random.fold_in(_rk, 2), (16, 128, 128), jnp.float32)
        return (x, txt)
    x, txt = _rec_inputs()

    def _L0_tok_setup():
        import jax, jax.numpy as jnp
        import numpy as np
        N_PATCHES = 8
        PATCH = 28
        C = 3
        IN_D = C * PATCH * PATCH
        HID = 128
        SEQ = N_PATCHES * N_PATCHES + 1

        def _positional_embedding(seq_len, dim):
            i = np.arange(seq_len)[:, None].astype(np.float32)
            j = np.arange(dim)[None, :].astype(np.float32)
            ang = i / np.power(100000.0, j / dim)
            pe = np.where(j % 2 == 0, np.sin(ang), np.cos(ang))
            return jnp.asarray(pe, dtype=jnp.float32)
        key = jax.random.key(seed)
        k1, k2, k3, k4 = jax.random.split(key, 4)
        B = 64
        X = jax.random.normal(k1, (B, C, 224, 224), dtype=jnp.float32)
        bound = 1.0 / np.sqrt(IN_D)
        W = jax.random.uniform(k2, (HID, IN_D), minval=-bound, maxval=bound, dtype=jnp.float32)
        b = jax.random.uniform(k3, (HID,), minval=-bound, maxval=bound, dtype=jnp.float32)
        class_token = jax.random.uniform(k4, (1, HID), dtype=jnp.float32)
        pos_embed = _positional_embedding(SEQ, HID)
        return {'X': X, 'W': W, 'b': b, 'class_token': class_token, 'pos_embed': pos_embed}
    _L0_tok_all = _L0_tok_setup()
    _L0_tok_in = {k: v for k, v in _L0_tok_all.items() if k in ('W', 'b', 'class_token', 'pos_embed')}
    del _L0_tok_all

    def _L0_attn_setup():
        import jax, jax.numpy as jnp
        import numpy as np
        B, N, C, H = (64, 200, 128, 8)
        D = C // H
        BASE = 10000.0

        def _rope(x):
            d = x.shape[-1]
            inv_freq = 1.0 / BASE ** (jnp.arange(0, d, 2, dtype=jnp.float32) / d)
            t = jnp.arange(x.shape[1], dtype=jnp.float32)
            freqs = jnp.outer(t, inv_freq)
            emb = jnp.concatenate([freqs, freqs], axis=-1)
            cos = jnp.cos(emb)[None, :, None, :]
            sin = jnp.sin(emb)[None, :, None, :]
            x1, x2 = (x[..., :d // 2], x[..., d // 2:])
            return x * cos + jnp.concatenate([-x2, x1], axis=-1) * sin
        key = jax.random.key(seed)
        k0, k1, k2 = jax.random.split(key, 3)
        x = jax.random.normal(k0, (B, N, C), jnp.float32)
        Wqk = jax.random.normal(k1, (C, 2 * C), jnp.float32) * C ** (-0.5)
        bqk = jnp.zeros((2 * C,), jnp.float32)
        lepe_w = jax.random.normal(k2, (C, 1, 3), jnp.float32) * 0.3
        lepe_b = jnp.zeros((C,), jnp.float32)
        return {'x': x, 'Wqk': Wqk, 'bqk': bqk, 'lepe_w': lepe_w, 'lepe_b': lepe_b}
    _L0_attn_all = _L0_attn_setup()
    _L0_attn_in = {k: v for k, v in _L0_attn_all.items() if k in ('Wqk', 'bqk', 'lepe_w', 'lepe_b')}
    del _L0_attn_all

    def _L0_ffn_setup():
        import jax, jax.numpy as jnp
        import numpy as np
        DIM = 128
        HID = 256
        E = 8
        K = 2
        B, S = (4, 512)
        key = jax.random.key(seed)
        ks = jax.random.split(key, 10)
        sd = DIM ** (-0.5)
        sh = HID ** (-0.5)
        return {'x': jax.random.normal(ks[0], (B, S, DIM), dtype=jnp.float32), 'gate_w': jax.random.normal(ks[1], (E, DIM), dtype=jnp.float32) * sd, 'biases': jnp.zeros((E,), dtype=jnp.float32), 'w1': jax.random.normal(ks[2], (E, DIM, HID), dtype=jnp.float32) * sd, 'w3': jax.random.normal(ks[3], (E, DIM, HID), dtype=jnp.float32) * sd, 'w2': jax.random.normal(ks[4], (E, HID, DIM), dtype=jnp.float32) * sh, 'sw1': jax.random.normal(ks[5], (DIM, HID), dtype=jnp.float32) * sd, 'sw3': jax.random.normal(ks[6], (DIM, HID), dtype=jnp.float32) * sd, 'sw2': jax.random.normal(ks[7], (HID, DIM), dtype=jnp.float32) * sh}
    _L0_ffn_all = _L0_ffn_setup()
    _L0_ffn_in = {k: v for k, v in _L0_ffn_all.items() if k in ('gate_w', 'biases', 'w1', 'w3', 'w2', 'sw1', 'sw3', 'sw2')}
    del _L0_ffn_all
    return {'x': x, 'txt': txt, 'L0_tok_W': _L0_tok_in['W'], 'L0_tok_b': _L0_tok_in['b'], 'L0_tok_class_token': _L0_tok_in['class_token'], 'L0_tok_pos_embed': _L0_tok_in['pos_embed'], 'L0_attn_Wqk': _L0_attn_in['Wqk'], 'L0_attn_bqk': _L0_attn_in['bqk'], 'L0_attn_lepe_w': _L0_attn_in['lepe_w'], 'L0_attn_lepe_b': _L0_attn_in['lepe_b'], 'L0_ffn_gate_w': _L0_ffn_in['gate_w'], 'L0_ffn_biases': _L0_ffn_in['biases'], 'L0_ffn_w1': _L0_ffn_in['w1'], 'L0_ffn_w3': _L0_ffn_in['w3'], 'L0_ffn_w2': _L0_ffn_in['w2'], 'L0_ffn_sw1': _L0_ffn_in['sw1'], 'L0_ffn_sw3': _L0_ffn_in['sw3'], 'L0_ffn_sw2': _L0_ffn_in['sw2']}

def reference(x, txt, L0_tok_W, L0_tok_b, L0_tok_class_token, L0_tok_pos_embed, L0_attn_Wqk, L0_attn_bqk, L0_attn_lepe_w, L0_attn_lepe_b, L0_ffn_gate_w, L0_ffn_biases, L0_ffn_w1, L0_ffn_w3, L0_ffn_w2, L0_ffn_sw1, L0_ffn_sw3, L0_ffn_sw2):
    import jax
    import jax.numpy as jnp

    def _L0_tok_ref(X, W, b, class_token, pos_embed):
        import jax, jax.numpy as jnp
        import numpy as np
        N_PATCHES = 8
        PATCH = 28
        C = 3
        IN_D = C * PATCH * PATCH
        HID = 128
        SEQ = N_PATCHES * N_PATCHES + 1

        def _positional_embedding(seq_len, dim):
            i = np.arange(seq_len)[:, None].astype(np.float32)
            j = np.arange(dim)[None, :].astype(np.float32)
            ang = i / np.power(100000.0, j / dim)
            pe = np.where(j % 2 == 0, np.sin(ang), np.cos(ang))
            return jnp.asarray(pe, dtype=jnp.float32)
        B = X.shape[0]
        patches = X.reshape(B, C, N_PATCHES, PATCH, N_PATCHES, PATCH)
        patches = patches.transpose(0, 2, 4, 1, 3, 5).reshape(B, N_PATCHES * N_PATCHES, IN_D)
        tokens = jnp.einsum('bpi,hi->bph', patches, W) + b
        cls = jnp.broadcast_to(class_token[None, :, :], (B, 1, HID))
        tokens = jnp.concatenate([cls, tokens], axis=1)
        return tokens * pos_embed[None, :, :]

    def _L0_attn_ref(x, Wqk, bqk, lepe_w, lepe_b):
        import jax, jax.numpy as jnp
        import numpy as np
        B, N, C, H = (64, 200, 128, 8)
        D = C // H
        BASE = 10000.0

        def _rope(x):
            d = x.shape[-1]
            inv_freq = 1.0 / BASE ** (jnp.arange(0, d, 2, dtype=jnp.float32) / d)
            t = jnp.arange(x.shape[1], dtype=jnp.float32)
            freqs = jnp.outer(t, inv_freq)
            emb = jnp.concatenate([freqs, freqs], axis=-1)
            cos = jnp.cos(emb)[None, :, None, :]
            sin = jnp.sin(emb)[None, :, None, :]
            x1, x2 = (x[..., :d // 2], x[..., d // 2:])
            return x * cos + jnp.concatenate([-x2, x1], axis=-1) * sin
        b, n, c = x.shape
        h, d = (H, C // H)
        qk = x @ Wqk + bqk
        q = jax.nn.elu(qk[..., :c]) + 1.0
        k = jax.nn.elu(qk[..., c:]) + 1.0
        qh = q.reshape(b, n, h, d)
        kh = k.reshape(b, n, h, d)
        vh = x.reshape(b, n, h, d)
        q_r = _rope(qh).transpose(0, 2, 1, 3)
        k_r = _rope(kh).transpose(0, 2, 1, 3)
        qh = qh.transpose(0, 2, 1, 3)
        kh = kh.transpose(0, 2, 1, 3)
        vh = vh.transpose(0, 2, 1, 3)
        kmean = kh.mean(axis=2)
        z = 1.0 / (jnp.einsum('bhnd,bhd->bhn', qh, kmean) + 1e-06)
        scale = n ** (-0.5)
        kv = jnp.einsum('bhnd,bhne->bhde', k_r * scale, vh * scale)
        out = jnp.einsum('bhnd,bhde->bhne', q_r, kv) * z[..., None]
        out = out.transpose(0, 2, 1, 3).reshape(b, n, c)
        v_ncw = x.transpose(0, 2, 1)
        lepe = jax.lax.conv_general_dilated(v_ncw, lepe_w, window_strides=(1,), padding=[(1, 1)], feature_group_count=c, dimension_numbers=('NCH', 'OIH', 'NCH'))
        lepe = lepe + lepe_b[None, :, None]
        return out + lepe.transpose(0, 2, 1)

    def _L0_ffn_ref(x, gate_w, biases, w1, w3, w2, sw1, sw3, sw2):
        import jax, jax.numpy as jnp
        import numpy as np
        DIM = 128
        HID = 256
        E = 8
        K = 2
        B, S = (4, 512)
        Bb, Ss, D = x.shape
        xt = x.reshape(Bb * Ss, D)
        shared = jax.nn.silu(xt @ sw1) * (xt @ sw3) @ sw2
        scores = xt @ gate_w.T
        _, idx = jax.lax.top_k(scores + biases, K)
        topv, _ = jax.lax.top_k(scores, K)
        p = jax.nn.sigmoid(topv)
        p = p / jnp.sum(p, axis=-1, keepdims=True)
        h = jax.nn.silu(jnp.einsum('td,edh->eth', xt, w1)) * jnp.einsum('td,edh->eth', xt, w3)
        y = jnp.einsum('eth,ehd->etd', h, w2)
        onehot = jax.nn.one_hot(idx, E, dtype=xt.dtype)
        comb = jnp.einsum('tk,tke->te', p, onehot)
        out = jnp.einsum('te,etd->td', comb, y) + shared
        return out.reshape(Bb, Ss, D)
    h = _L0_tok_ref(x, L0_tok_W, L0_tok_b, L0_tok_class_token, L0_tok_pos_embed)
    h = jnp.concatenate([h, txt], axis=1)
    h = h + _L0_attn_ref(_layernorm(h, axis=-1), L0_attn_Wqk, L0_attn_bqk, L0_attn_lepe_w, L0_attn_lepe_b)
    h = h + _L0_ffn_ref(_layernorm(h, axis=-1), L0_ffn_gate_w, L0_ffn_biases, L0_ffn_w1, L0_ffn_w3, L0_ffn_w2, L0_ffn_sw1, L0_ffn_sw3, L0_ffn_sw2)
    return h

_drawn_inputs = setup_inputs


def setup_inputs(seed=0):
    import zlib

    import numpy as np

    out = dict(_drawn_inputs(seed))
    spreads = {'L0_attn_bqk': (0.0, 0.299), 'L0_attn_lepe_b': (0.0, 0.1), 'L0_ffn_biases': (0.0, 0.1)}
    factors = {}
    for name, (base, spread) in spreads.items():
        noise = np.random.default_rng([zlib.crc32(name.encode()), seed]).standard_normal(out[name].shape)
        drawn = base * np.exp(spread * noise) if base else spread * noise
        out[name] = jnp.asarray(drawn.astype(out[name].dtype))
    for name, factor in factors.items():
        out[name] = (out[name] * factor).astype(out[name].dtype)
    return out
```

```python
import numpy as np
import concourse.bass as bass
from concourse import mybir
from contextlib import ExitStack

F32 = mybir.dt.float32
I32 = mybir.dt.int32
U32 = mybir.dt.uint32
ALU = mybir.AluOpType
ACT = mybir.ActivationFunctionType
AX = mybir.AxisListType

P = 128
B, CH, IMG, GRID = 16, 3, 224, 8
PATCH = IMG // GRID
IN_D = CH * PATCH * PATCH
KB = IN_D // P
KR = IN_D - KB * P
D = 128
NP_, NT = GRID * GRID, 128
SEQ = 1 + NP_ + NT
NTOK = B * SEQ
H, HD = 8, 16
G = B // 2
GN = 2 * SEQ
LN_EPS, Z_EPS = 1e-5, 1e-6
E, HID = 8, 256
PIECES = [(0, 1 + NP_, 0), (1 + NP_, NT, 1), (SEQ, 1 + NP_, 0), (SEQ + 1 + NP_, NT, 1)]
J = -(-NTOK // P)
LAST = NTOK - (J - 1) * P
CAP = NTOK + P
TILES = (2 * NTOK - E) // P + E
DEAD = TILES - (2 * NTOK) // P
ROW = D + 2
BIG = 1 << 20
U = 4
assert TILES % U == 0 and G % 2 == 0

C_ID, C_MEAN, C_TRI, C_ONE, C_MASK = 0, P, 2 * P, 3 * P, 4 * P
C_COS, C_SIN = 5 * P, 5 * P + 4 * P
C_RANK, C_TILE, C_RESET = 13 * P, 13 * P + 8, 14 * P
C_BASE = C_RESET + E * J
C_IOTA = C_BASE + E
NCONST = C_IOTA + TILES


def constants():
    c = np.zeros((P, NCONST), np.float32)
    c[:, C_ID:C_ID + P] = np.eye(P)
    c[:, C_MEAN:C_MEAN + P] = 1.0 / D
    c[:, C_TRI:C_TRI + P] = np.triu(np.ones((P, P)), 1)
    c[:, C_ONE:C_ONE + P] = 1.0
    head = np.arange(P) // HD
    c[:, C_MASK:C_MASK + P] = (head[:, None] == head[None, :]) / SEQ
    inv = 1.0 / 10000.0 ** (np.arange(0, HD, 2, dtype=np.float32) / HD)
    freq = np.outer(np.arange(SEQ, dtype=np.float32), inv).astype(np.float32)
    cos, sin = np.cos(freq), np.sin(freq)
    for half, (start, rows) in enumerate(((0, 1 + NP_), (1 + NP_, NT))):
        at = slice(start, start + rows)
        c[:rows, C_COS + 256 * half:C_COS + 256 * half + 256] = np.tile(np.concatenate([cos[at], cos[at]], 1), (1, 16))
        c[:rows, C_SIN + 256 * half:C_SIN + 256 * half + 256] = np.tile(np.concatenate([-sin[at], sin[at]], 1), (1, 16))
    c[:, C_RANK:C_RANK + E] = np.arange(E, 0, -1)
    reset = np.ones((E, J))
    reset[:, 0] = 0
    c[:, C_RESET:C_RESET + E * J] = reset.reshape(-1)
    c[:, C_BASE:C_BASE + E] = np.arange(E) * CAP
    c[:, C_IOTA:C_IOTA + TILES] = np.arange(TILES)
    return c


def destinations():
    flat = np.arange(J)[None, :, None] * P + np.arange(P)[:, None, None]
    ids = flat + np.arange(2)[None, None, :] * NTOK
    return np.concatenate([ids.reshape(P, 2 * J), np.full((P, 1), BIG)], 1).astype(np.int32)


def build(nc, patches, txt, w_tok, b_tok, cls, pos, wqk, bqk, lepe_w, lepe_b, gate_w, gate_b,
          w1, w3, w2, sw1, sw3, sw2, consts, dests, out):
    xs_dram = nc.dram_tensor("xs_dram", [E * CAP + DEAD * P, ROW], F32).ap()
    y_dram = nc.dram_tensor("y_dram", [2 * NTOK, D], F32).ap()
    ctx = ExitStack()
    with ctx:
        def sb(name, shape, dt=F32):
            return ctx.enter_context(nc.sbuf_tensor(name, shape, dt))

        def pb(name):
            return ctx.enter_context(nc.psum_tensor(name, [P, 512], F32))

        def sem(name):
            return ctx.enter_context(nc.semaphore(name))

        def sems(name, n):
            return [sem(f"{name}{i}") for i in range(n)]

        cst = sb("cst", [P, NCONST])
        ident, mean_w = cst[:, C_ID:C_ID + P], cst[:, C_MEAN:C_MEAN + P]
        tri, ones, mask = cst[:, C_TRI:C_TRI + P], cst[:, C_ONE:C_ONE + P], cst[:, C_MASK:C_MASK + P]
        dest_sb = sb("dest_sb", [P, 2 * J + 1], I32)
        wt = sb("wt", [P, KB, D])
        wt_rest = sb("wt_rest", [KR, D])
        cols = sb("cols", [P, 8])
        pos_sb = sb("pos_sb", [P, 1 + NP_])
        wqk_sb = sb("wqk_sb", [P, 2 * D])
        bqk_sb = sb("bqk_sb", [P, 2 * D])
        gate_sb = sb("gate_sb", [P, E])
        gateb_sb = sb("gateb_sb", [P, E])
        w13 = sb("w13", [P, E, 2 * HID])
        w2_sb = sb("w2_sb", [P, E, 2, D])
        sw13 = sb("sw13", [P, 2 * HID])
        sw2_sb = sb("sw2_sb", [P, 2, D])

        xp = [sb(f"xp{i}", [P, KB, P]) for i in range(2)]
        xr = [sb(f"xr{i}", [KR, P]) for i in range(2)]
        hT = [sb(f"hT{i}", [P, 2, SEQ]) for i in range(2)]
        dev1, sq1, lv1, rs1 = (sb(n, [P, GN]) for n in ("dev1", "sq1", "lv1", "rs1"))
        dev2, sq2, lv2, rs2 = (sb(n, [P, GN]) for n in ("dev2", "sq2", "lv2", "rs2"))
        xT = [sb(f"xT{i}", [P, 2, SEQ]) for i in range(2)]
        att = sb("att", [P, 5, 4, 2 * D])
        qk, ex, rl, ft, rr = ([att[:, i, k, :] for k in range(4)] for i in range(5))
        cc, ss = ex, rl
        vt = [sb(f"vt{k}", [P, D]) for k in range(4)]
        qq = [sb(f"qq{j}", [P, 2, SEQ]) for j in range(2)]
        kvm = [sb(f"kvm{j}", [P, 2, D]) for j in range(2)]
        zt = [sb(f"zt{j}", [P, SEQ]) for j in range(2)]
        zr = [sb(f"zr{j}", [P, SEQ]) for j in range(2)]
        ot = sb("ot", [P, 2, SEQ])
        hl = [sb(f"hl{i}", [P, 2, SEQ]) for i in range(2)]
        h2T = sb("h2T", [P, NTOK])
        x2T = sb("x2T", [P, NTOK])

        bank = [pb(f"bank{i}") for i in range(8)]
        ps_ln1, ps_ln2, ps_tok = bank[0], bank[1], bank[2]
        ps_qkv, ps_tr, ps_kv, ps_od = bank[3:5], bank[5], bank[6], bank[7]

        sc = sb("sc", [P, J, E])
        scb = sb("scb", [P, J, E])
        eq = sb("eq", [P, J, E])
        wk = sb("wk", [P, J, E])
        pick = sb("pick", [P, 2, J, E])
        pick_u = sb("pick_u", [P, J, E])
        top = sb("top", [P, 2, J])
        mx = sb("mx", [P, J])
        rk = sb("rk", [P, J])
        sg = sb("sg", [P, 2, J])
        both = sb("both", [P, J, E])
        cnt = sb("cnt", [P, E, J])
        inc = sb("inc", [P, E, J])
        exc = sb("exc", [P, E, J])
        place = sb("place", [P, J, E])
        prod = sb("prod", [P, 2, J, E])
        pos_f = sb("pos_f", [P, 2, J])
        pos_i = sb("pos_i", [P, 2, J], I32)
        tn = sb("tn", [P, E])
        ti = sb("ti", [P, 2, E], I32)
        tf = sb("tf", [P, E])
        te = sb("te", [P, E])
        ge = sb("ge", [P, TILES, E])
        gn = sb("gn", [P, TILES, E])
        t_e = sb("t_e", [P, TILES])
        t_s = sb("t_s", [P, TILES])
        t_r = sb("t_r", [P, 2, TILES])
        tab_e = sb("tab_e", [P, TILES], I32)
        tab_r = sb("tab_r", [P, TILES], I32)
        tab_p = sb("tab_p", [P, E], I32)
        xd = sb("xd", [P, J, 2, ROW])
        pad = sb("pad", [P, ROW])

        xs = [sb(f"xs{u}", [P, ROW]) for u in range(U)]
        xsT = [sb(f"xsT{u}", [P, P]) for u in range(2)]
        hs = [sb(f"hs{u}", [P, HID]) for u in range(2)]
        hm = [sb(f"hm{u}", [P, HID]) for u in range(2)]
        hmT = [sb(f"hmT{u}", [P, 2, P]) for u in range(2)]
        ys = [sb(f"ys{u}", [P, D]) for u in range(U)]
        sh_s = [dev1, sq1]
        sh_h = [dev2, sq2]
        YC = 5
        ya = [xp[i][:, 0:YC, :] for i in range(2)]
        yb = [xp[i][:, YC:2 * YC, :] for i in range(2)]
        res = att[:].rearrange("p a k c -> p (a k c)")[:, 0:J * D].rearrange("p (j d) -> p j d", d=D)

        s_cst, s_wtok, s_small, s_wexp = sem("s_cst"), sem("s_wtok"), sem("s_small"), sem("s_wexp")
        x_loaded, txt_loaded = sems("x_loaded", 2), sems("txt_loaded", 2)
        cls_ready = sem("cls_ready")
        tok_done, hpatch_done = sem("tok_done"), sem("hpatch_done")
        mean1, dev1_done, sq1_done, var1, lv1_done, rs1_done = (
            sem(n) for n in ("mean1", "dev1_done", "sq1_done", "var1", "lv1_done", "rs1_done"))
        mean2, dev2_done, sq2_done, var2, lv2_done, rs2_done = (
            sem(n) for n in ("mean2", "dev2_done", "sq2_done", "var2", "lv2_done", "rs2_done"))
        xT_done, x2_done = sem("xT_done"), sem("x2_done")
        qkv_done, qk_done, v_done = sems("qkv_done", 4), sems("qk_done", 4), sems("v_done", 4)
        ex_done, rl_done, ft_done = sems("ex_done", 4), sems("rl_done", 4), sems("ft_done", 4)
        cc_done, ss_done, rr_done = sems("cc_done", 4), sems("ss_done", 4), sems("rr_done", 4)
        qT_done, qq_done = sems("qT_done", 2), sems("qq_done", 2)
        kv_done, kvm_done, od_done = sems("kv_done", 2), sems("kvm_done", 2), sems("od_done", 2)
        zt_done, zr_done, ot_done = sems("zt_done", 2), sems("zr_done", 2), sems("ot_done", 2)
        lc_done, lh_done, tap_done, hl_done, h2_done = (
            sem(n) for n in ("lc_done", "lh_done", "tap_done", "hl_done", "h2_done"))
        ids_ready, pad_ready = sem("ids_ready"), sem("pad_ready")
        gate_done, sc_done, route, sg_e, both_ready, pref_done, pos_done = (
            sem(n) for n in ("gate_done", "sc_done", "route", "sg_e", "both_ready", "pref_done", "pos_done"))
        weight_done, tab_done, route_chain = sem("weight_done"), sem("tab_done"), sem("route_chain")
        xd_tr, xd_copied = sem("xd_tr"), sem("xd_copied")
        xd_ready = sem("xd_ready")
        scattered, padded = sem("scattered"), sem("padded")
        sh_up, sh_act, sh_mul, sh_down, sh_add = (
            sem(n) for n in ("sh_up", "sh_act", "sh_mul", "sh_down", "sh_add"))
        res_tr, res_copied = sem("res_tr"), sem("res_copied")
        xs_loaded = sems("xs_loaded", U)
        tx_done, xsT_done, up_done, silu_done, hm_done, th_done, hmT_done, dn_done, ys_done = (
            sem(n) for n in ("tx_done", "xsT_done", "up_done", "silu_done", "hm_done", "th_done",
                             "hmT_done", "dn_done", "ys_done"))
        y_sent = sems("y_sent", U)
        y_loaded, fin_a, fin_done, out_sent = sems("y_loaded", 2), sem("fin_a"), sem("fin_done"), sems("out_sent", 2)

        block = ctx.enter_context(nc.Block())

        def after(eng, s, value):
            if not isinstance(value, int) or value > 0:
                eng.wait_ge(s, value)

        def two(eng, body):
            body(0, 0)
            with eng.Fori(0, G // 2 - 1) as i:
                n = eng.snap(i)
                body(1, n)
                body(0, n + 1)
            body(1, G // 2 - 1)

        @block.sync
        def _(sp):
            def load_group(p, n):
                g = 2 * n + p
                at, rest, tokens, old = [
                    v if isinstance(v, int) else sp.snap(v)
                    for v in (g * IN_D, g * IN_D + KB * P, g * 2 * NT, g - 1)]
                after(sp, tok_done, old)
                sp.dma_start(xp[p][:], patches[bass.ds(at, KB * P), :].rearrange(
                    "(q k) t -> q k t", k=KB)).then_inc(x_loaded[p], 16)
                sp.dma_start(xr[p][:], patches[bass.ds(rest, KR), :]).then_inc(x_loaded[p], 16)
                after(sp, h2_done, old)
                sp.dma_start(hT[p][:, :, 1 + NP_:SEQ], txt[:, bass.ds(tokens, 2 * NT)].rearrange(
                    "c (b t) -> c b t", b=2)).then_inc(txt_loaded[p], 16)

            sp.dma_start(wt[:], w_tok[0:KB * P, :].rearrange("(q k) h -> q k h", k=KB)).then_inc(s_wtok, 16)
            sp.dma_start(wt_rest[:], w_tok[KB * P:IN_D, :]).then_inc(s_wtok, 16)
            two(sp, load_group)

            sp.wait_ge(pad_ready, 2)
            sp.dma_start(xs_dram[E * CAP:, :].rearrange("(k q) r -> q k r", q=P),
                         pad[:].rearrange("p (o r) -> p o r", o=1).broadcast_to([P, DEAD, ROW])
                         ).then_inc(padded, 16)
            sp.wait_ge(tab_done, 1)
            for e in range(E):
                row = sp.value_load(tab_p[0:1, e:e + 1], min_val=0, max_val=E * CAP - P)
                sp.dma_start(xs_dram[bass.ds(row, P), :], pad[:]).then_inc(padded, 16)

            sp.wait_ge(scattered, 16 * 2 * J)
            sp.wait_ge(padded, 16 * (E + 1))

            used_reg, sent_reg = sp.alloc_register("used"), sp.alloc_register("sent")

            def load_tiles(n):
                for u in range(U):
                    t = U * n + u
                    row = sp.value_load(tab_r[0:1, bass.ds(t, 1)], min_val=0, max_val=E * CAP)
                    used = t - U + 1
                    sent = 16 * n
                    if not isinstance(n, int):
                        sp.reg_mov(used_reg, used)
                        sp.reg_mov(sent_reg, sent)
                        used, sent = used_reg, sent_reg
                    after(sp, ys_done, used)
                    after(sp, y_sent[u], sent)
                    sp.dma_start(xs[u][:], xs_dram[bass.ds(row, P), :]).then_inc(xs_loaded[u], 16)

            load_tiles(0)
            with sp.Fori(1, TILES // U) as n:
                load_tiles(sp.snap(n))

            for u in range(U):
                sp.wait_ge(y_sent[u], 16 * (TILES // U))
            for c in range(J // YC):
                rows = YC * P if c < J // YC - 1 else (YC - 1) * P
                after(sp, out_sent[c % 2], (c // 2) * 16)
                for k, y in enumerate((ya, yb)):
                    at = k * NTOK + c * YC * P
                    sp.dma_start(y[c % 2][:, 0:rows // P, :], y_dram[at:at + rows, :].rearrange(
                        "(j q) d -> q j d", q=P)).then_inc(y_loaded[c % 2], 16)
                    if rows < YC * P:
                        sp.dma_start(y[c % 2][0:LAST, YC - 1, :], y_dram[at + rows:at + rows + LAST, :]
                                     ).then_inc(y_loaded[c % 2], 16)

        @block.scalar
        def _(act):
            A = nc.scalar.activation
            act.dma_start(cst[:], consts[:, :]).then_inc(s_cst, 16)
            act.dma_start(cols[:, 0:1], b_tok[:, :]).then_inc(s_small, 16)
            act.dma_start(cols[:, 1:2], cls[:, :]).then_inc(s_small, 16)
            act.dma_start(cols[:, 2:3], lepe_b[:, :]).then_inc(s_small, 16)
            act.dma_start(cols[:, 3:6], lepe_w[:, :]).then_inc(s_small, 16)
            act.dma_start(pos_sb[:], pos[:, :]).then_inc(s_small, 16)
            act.dma_start(wqk_sb[:], wqk[:, :]).then_inc(s_small, 16)
            act.dma_start(bqk_sb[:], bqk[:, :].broadcast_to([P, 2 * D])).then_inc(s_small, 16)
            act.dma_start(gate_sb[:], gate_w[:, :]).then_inc(s_small, 16)
            act.dma_start(gateb_sb[:], gate_b[:, :].broadcast_to([P, E])).then_inc(s_small, 16)
            act.dma_start(dest_sb[:], dests[:, :]).then_inc(s_small, 16)

            def square1(g):
                act.wait_ge(dev1_done, g + 1)
                A(sq1[:], dev1[:], ACT.Square).then_inc(sq1_done, 1)

            def rstd1(g):
                act.wait_ge(var1, g + 1)
                A(lv1[:], ps_ln1[:, 0:GN], ACT.Ln, bias=LN_EPS).then_inc(lv1_done, 1)
                act.wait_ge(lv1_done, g + 1)
                A(rs1[:], lv1[:], ACT.Exp, scale=-0.5).then_inc(rs1_done, 1)

            def square2(g):
                act.wait_ge(dev2_done, g + 1)
                A(sq2[:], dev2[:], ACT.Square).then_inc(sq2_done, 1)

            def rstd2(g):
                act.wait_ge(var2, g + 1)
                A(lv2[:], ps_ln2[:, 0:GN], ACT.Ln, bias=LN_EPS).then_inc(lv2_done, 1)
                act.wait_ge(lv2_done, g + 1)
                A(rs2[:], lv2[:], ACT.Exp, scale=-0.5).then_inc(rs2_done, 1)

            def piece(g, k):
                n = PIECES[k][1]
                act.wait_ge(qk_done[k], g + 1)
                after(act, kv_done[k // 2], g)
                nc.scalar.copy(vt[k][0:n, :], ps_qkv[k % 2][0:n, 2 * D:3 * D]).then_inc(v_done[k], 1)
                A(ex[k][0:n, :], qk[k][0:n, :], ACT.Exp).then_inc(ex_done[k], 1)
                A(rl[k][0:n, :], qk[k][0:n, :], ACT.Relu).then_inc(rl_done[k], 1)

            def queries(g, j):
                act.wait_ge(qT_done[j], g + 1)
                after(act, od_done[j], g)
                nc.scalar.copy(qq[j][:], ps_tr[:, 0:GN]).then_inc(qq_done[j], 1)

            def group(p, n, first=False, last=False):
                g = 2 * n + p
                piece(g, 0)
                after(act, h2_done, g - 1)
                act.wait_ge(xT_done, g + 1)
                A(hl[p][:], xT[p][:], ACT.Identity, bias=cols[:, 2:3], scale=cols[:, 4:5]).then_inc(lc_done, 1)
                piece(g, 1)
                piece(g, 2)
                if not first:
                    square2(g - 1)
                piece(g, 3)
                if not first:
                    rstd2(g - 1)
                queries(g, 0)
                if not last:
                    square1(g + 1)
                queries(g, 1)
                if not last:
                    rstd1(g + 1)

            act.wait_ge(s_small, 160)
            square1(0)
            rstd1(0)
            act.dma_start(sw13[:, 0:HID], sw1[:, :]).then_inc(s_wexp, 16)
            act.dma_start(sw13[:, HID:2 * HID], sw3[:, :]).then_inc(s_wexp, 16)
            act.dma_start(sw2_sb[:], sw2.rearrange("(k q) d -> q k d", q=P)).then_inc(s_wexp, 16)
            act.dma_start(w13[:, :, 0:HID], w1.rearrange("e d h -> d e h")).then_inc(s_wexp, 16)
            act.dma_start(w13[:, :, HID:2 * HID], w3.rearrange("e d h -> d e h")).then_inc(s_wexp, 16)
            act.dma_start(w2_sb[:], w2.rearrange("e (k q) d -> q e k d", q=P)).then_inc(s_wexp, 16)
            group(0, 0, first=True)
            with act.Fori(0, G // 2 - 1) as i:
                n = act.snap(i)
                group(1, n)
                group(0, n + 1)
            group(1, G // 2 - 1, last=True)
            square2(G - 1)
            rstd2(G - 1)

            act.wait_ge(route, 1)
            A(sg[:], top[:], ACT.Exp, scale=-1.0).then_inc(sg_e, 1)

            with act.Fori(0, G) as i:
                g = act.snap(i)
                for m in range(2):
                    act.wait_ge(sh_up, 2 * g + m + 1)
                    act.wait_ge(sh_mul, 2 * g + m)
                    A(sh_s[m][:], bank[m][:, 0:GN], ACT.Silu).then_inc(sh_act, 1)
            for j in range(J):
                rows = P if j < J - 1 else LAST
                act.wait_ge(res_tr, j + 1)
                nc.scalar.copy(res[0:rows, j, :], bank[6 + j % 2][0:rows, 0:D]).then_inc(res_copied, 1)

            def gelu(t, q):
                act.wait_ge(up_done, t + 1)
                after(act, hm_done, t - 1)
                A(hs[q][:], bank[2 + q][:, 0:HID], ACT.Silu).then_inc(silu_done, 1)

            def turned(t, q):
                act.wait_ge(th_done, t + 1)
                after(act, dn_done, t - 1)
                nc.scalar.copy(hmT[q][:], bank[4 + q][:, 0:HID]).then_inc(hmT_done, 1)

            def result(t, q, u, n):
                act.wait_ge(dn_done, t + 1)
                after(act, y_sent[u], 16 * n)
                A(ys[u][:], bank[6 + q][:, 0:D], ACT.Copy, scale=xs[u][:, D + 1:D + 2]).then_inc(ys_done, 1)

            def tiles(n, first=False):
                for u in range(U):
                    t = U * n + u
                    if not (first and u < 1):
                        turned(t - 1, (u - 1) % 2)
                    gelu(t, u % 2)
                    if not (first and u < 2):
                        result(t - 2, u % 2, (u - 2) % U, n if u >= 2 else n - 1)

            tiles(0, first=True)
            with act.Fori(1, TILES // U) as n:
                tiles(act.snap(n))
            turned(TILES - 1, 1)
            result(TILES - 2, 0, U - 2, TILES // U - 1)
            result(TILES - 1, 1, U - 1, TILES // U - 1)

            for c in range(J // YC):
                act.wait_ge(fin_done, c + 1)
                rows = YC * P if c < J // YC - 1 else (YC - 1) * P
                at = c * YC * P
                act.dma_start(out[at:at + rows, :].rearrange("(j q) d -> q j d", q=P),
                              ya[c % 2][:, 0:rows // P, :]).then_inc(out_sent[c % 2], 16)
                if rows < YC * P:
                    act.dma_start(out[at + rows:NTOK, :], ya[c % 2][0:LAST, YC - 1, :]
                                  ).then_inc(out_sent[c % 2], 16)
            n_even, n_odd = (J // YC + 1) // 2, (J // YC) // 2
            act.wait_ge(out_sent[0], 16 * (n_even + ((J // YC) % 2)))
            act.wait_ge(out_sent[1], 16 * (n_odd + 1 - ((J // YC) % 2)))

        @block.gpsimd
        def _(pool):
            pool.wait_ge(s_cst, 16)
            pool.wait_ge(s_small, 160)
            nc.gpsimd.memset(pad[:], 0.0).then_inc(pad_ready, 1)
            pool.wait_ge(pad_ready, 1)
            nc.gpsimd.tensor_copy(pad[:, D:D + 1].bitcast(I32), dest_sb[:, 2 * J:2 * J + 1]).then_inc(pad_ready, 1)
            nc.gpsimd.tensor_copy(xd[:, :, :, D:D + 1].bitcast(I32),
                                  dest_sb[:, 0:2 * J].rearrange("p (j k o) -> p j k o", k=2, o=1)
                                  ).then_inc(ids_ready, 1)

            def group(p, n):
                g = 2 * n + p
                for k in range(4):
                    rows, half = PIECES[k][1], PIECES[k][2]
                    pool.wait_ge(ft_done[k], g + 1)
                    after(pool, rr_done[k], g)
                    sin = cst[0:rows, C_SIN + 256 * half:C_SIN + 256 * half + 256]
                    nc.gpsimd.tensor_tensor(
                        ss[k][0:rows, :].rearrange("p (h t e) -> p h t e", t=2, e=8),
                        ft[k][0:rows, :].rearrange("p (h t e) -> p h t e", t=2, e=8)[:, :, ::-1, :],
                        sin.rearrange("p (h t e) -> p h t e", t=2, e=8), ALU.mult).then_inc(ss_done[k], 1)
                    if k == 0:
                        pool.wait_ge(lc_done, g + 1)
                        nc.gpsimd.tensor_tensor(hl[p][:], hl[p][:], hT[p][:], ALU.add).then_inc(lh_done, 1)

            two(pool, group)

            for j in range(J):
                rows = P if j < J - 1 else LAST
                pool.wait_ge(xd_ready, j + 1)
                if j == 0:
                    pool.wait_ge(pos_done, 1)
                    pool.wait_ge(weight_done, 1)
                for k in range(2):
                    nc.gpsimd.indirect_dma_start(
                        out=xs_dram[:, :], out_offset=bass.IndirectOffsetOnAxis(ap=pos_i[0:rows, k, j:j + 1], axis=0),
                        in_=xd[0:rows, j, k, :], in_offset=None).then_inc(scattered, 16)

            bound_reg = pool.alloc_register("bound")
            pool.reg_mov(bound_reg, 2 * NTOK - 1)
            bound = pool.snap(bound_reg)
            count = pool.alloc_register("count")
            pool.reg_mov(count, 1)

            def send(u):
                pool.wait_ge(ys_done, count)
                pool.reg_add(count, count, 1)
                nc.gpsimd.indirect_dma_start(
                    out=y_dram[:, :], out_offset=bass.IndirectOffsetOnAxis(ap=xs[u][:, D:D + 1].bitcast(I32), axis=0),
                    in_=ys[u][:], in_offset=None, bounds_check=bound, oob_is_err=False).then_inc(y_sent[u], 16)

            with pool.Fori(0, TILES // U):
                for u in range(U):
                    send(u)

        @block.vector
        def _(dve):
            V = nc.vector

            def patch(p, n):
                g = 2 * n + p
                dve.wait_ge(tok_done, g + 1)
                after(dve, lh_done, g - 1)
                V.scalar_tensor_tensor(
                    out=hT[p][:, :, 1:1 + NP_], in0=ps_tok[:, 0:P].rearrange("p (b t) -> p b t", b=2),
                    scalar=cols[:, 0:1],
                    in1=pos_sb[:, 1:1 + NP_].rearrange("p (o t) -> p o t", o=1).broadcast_to([P, 2, NP_]),
                    op0=ALU.add, op1=ALU.mult).then_inc(hpatch_done, 1)

            def center1(p, n):
                g = 2 * n + p
                dve.wait_ge(mean1, g + 1)
                V.tensor_tensor(dev1[:].rearrange("p (b t) -> p b t", b=2), hT[p][:],
                                ps_ln1[:, 0:GN].rearrange("p (b t) -> p b t", b=2), ALU.subtract
                                ).then_inc(dev1_done, 1)

            def norm1(p, n):
                g = 2 * n + p
                dve.wait_ge(rs1_done, g + 1)
                after(dve, qkv_done[3], g - 1)
                V.tensor_tensor(xT[p][:].rearrange("p b t -> p (b t)"), dev1[:], rs1[:], ALU.mult).then_inc(xT_done, 1)

            def center2(p, n):
                g = 2 * n + p
                dve.wait_ge(mean2, g + 1)
                V.tensor_tensor(dev2[:], h2T[:, bass.ds(g * GN, GN)], ps_ln2[:, 0:GN], ALU.subtract
                                ).then_inc(dev2_done, 1)

            def norm2(p, n):
                g = 2 * n + p
                dve.wait_ge(rs2_done, g + 1)
                V.tensor_tensor(x2T[:, bass.ds(g * GN, GN)], dev2[:], rs2[:], ALU.mult).then_inc(x2_done, 1)

            def bias(g, k):
                n = PIECES[k][1]
                dve.wait_ge(qkv_done[k], g + 1)
                V.tensor_tensor(qk[k][0:n, :], ps_qkv[k % 2][0:n, 0:2 * D], bqk_sb[0:n, :], ALU.add
                                ).then_inc(qk_done[k], 1)

            def elu(g, k):
                n = PIECES[k][1]
                dve.wait_ge(ex_done[k], g + 1)
                dve.wait_ge(rl_done[k], g + 1)
                after(dve, kv_done[k // 2], g)
                after(dve, ss_done[k], g)
                V.scalar_tensor_tensor(out=ft[k][0:n, :], in0=ex[k][0:n, :], scalar=1.0, in1=rl[k][0:n, :],
                                       op0=ALU.min, op1=ALU.add).then_inc(ft_done[k], 1)

            def cosine(g, k):
                n, half = PIECES[k][1], PIECES[k][2]
                dve.wait_ge(ft_done[k], g + 1)
                V.tensor_tensor(cc[k][0:n, :], ft[k][0:n, :], cst[0:n, C_COS + 256 * half:C_COS + 256 * half + 256],
                                ALU.mult).then_inc(cc_done[k], 1)

            def rotated(g, k):
                n = PIECES[k][1]
                dve.wait_ge(cc_done[k], g + 1)
                dve.wait_ge(ss_done[k], g + 1)
                V.tensor_tensor(rr[k][0:n, :], cc[k][0:n, :], ss[k][0:n, :], ALU.add).then_inc(rr_done[k], 1)

            def heads(g, j):
                dve.wait_ge(kv_done[j], g + 1)
                after(dve, od_done[j], g)
                V.tensor_tensor(kvm[j][:, 0, :], ps_kv[:, 0:D], mask, ALU.mult)
                V.tensor_scalar(kvm[j][:, 1, :], mask, ps_kv[:, D:D + 1], None, ALU.mult).then_inc(kvm_done[j], 1)

            def attended(g, j):
                dve.wait_ge(od_done[j], g + 1)
                V.tensor_scalar(zt[j][:], ps_od[:, SEQ:2 * SEQ], Z_EPS, None, ALU.add).then_inc(zt_done[j], 1)
                dve.wait_ge(zt_done[j], g + 1)
                V.reciprocal(zr[j][:], zt[j][:]).then_inc(zr_done[j], 1)
                dve.wait_ge(zr_done[j], g + 1)
                V.tensor_tensor(ot[:, j, :], ps_od[:, 0:SEQ], zr[j][:], ALU.mult).then_inc(ot_done[j], 1)

            def taps(p, n):
                g = 2 * n + p
                dve.wait_ge(lh_done, g + 1)
                V.scalar_tensor_tensor(out=hl[p][:, :, 1:SEQ], in0=xT[p][:, :, 0:SEQ - 1], scalar=cols[:, 3:4],
                                       in1=hl[p][:, :, 1:SEQ], op0=ALU.mult, op1=ALU.add).then_inc(tap_done, 1)
                dve.wait_ge(tap_done, g + 1)
                V.scalar_tensor_tensor(out=hl[p][:, :, 0:SEQ - 1], in0=xT[p][:, :, 1:SEQ], scalar=cols[:, 5:6],
                                       in1=hl[p][:, :, 0:SEQ - 1], op0=ALU.mult, op1=ALU.add).then_inc(hl_done, 1)

            def add(p, n):
                g = 2 * n + p
                dve.wait_ge(hl_done, g + 1)
                dve.wait_ge(ot_done[0], g + 1)
                dve.wait_ge(ot_done[1], g + 1)
                V.tensor_tensor(h2T[:, bass.ds(g * GN, GN)].rearrange("p (b t) -> p b t", b=2), ot[:], hl[p][:],
                                ALU.add).then_inc(h2_done, 1)

            def group(p, n, first=False, last=False):
                g = 2 * n + p
                before = (1 - p, n - 1 if p == 0 else n)
                behind = (1 - p, n if p == 0 else n + 1)
                bias(g, 0)
                bias(g, 1)
                elu(g, 0)
                cosine(g, 0)
                bias(g, 2)
                elu(g, 1)
                cosine(g, 1)
                bias(g, 3)
                rotated(g, 0)
                elu(g, 2)
                cosine(g, 2)
                if not first:
                    center2(*before)
                rotated(g, 1)
                elu(g, 3)
                cosine(g, 3)
                rotated(g, 2)
                if not last:
                    patch(*behind)
                heads(g, 0)
                rotated(g, 3)
                if not last:
                    center1(*behind)
                if not first:
                    norm2(*before)
                taps(p, n)
                heads(g, 1)
                attended(g, 0)
                if not last:
                    norm1(*behind)
                attended(g, 1)
                add(p, n)

            dve.wait_ge(s_small, 160)
            dve.wait_ge(s_cst, 16)
            for i in range(2):
                V.tensor_tensor(hT[i][:, :, 0], cols[:, 1:2].broadcast_to([P, 2]),
                                pos_sb[:, 0:1].broadcast_to([P, 2]), ALU.mult).then_inc(cls_ready, 1)
            V.memset(sc[:], 0.0).then_inc(cls_ready, 1)
            patch(0, 0)
            center1(0, 0)
            norm1(0, 0)
            group(0, 0, first=True)
            with dve.Fori(0, G // 2 - 1) as i:
                n = dve.snap(i)
                group(1, n)
                group(0, n + 1)
            group(1, G // 2 - 1, last=True)
            center2(1, G // 2 - 1)
            norm2(1, G // 2 - 1)

            steps = [0]
            chain = route_chain

            def then(ins):
                steps[0] += 1
                ins.then_inc(chain, 1)
                dve.wait_ge(chain, steps[0])

            def per_tile(ap):
                return ap.rearrange("p (j o) -> p j o", o=1).broadcast_to([P, J, E])

            def per_expert(ap):
                return ap.rearrange("p (o e) -> p o e", o=1).broadcast_to([P, J, E])

            def first_best(scores, best, one_hot):
                then(V.tensor_reduce(best, scores, AX.X, ALU.max))
                then(V.tensor_tensor(eq[:], scores, per_tile(best), ALU.is_equal))
                then(V.tensor_tensor(wk[:], eq[:], per_expert(cst[:, C_RANK:C_RANK + E]), ALU.mult))
                then(V.tensor_reduce(rk[:], wk[:], AX.X, ALU.max))
                then(V.tensor_tensor(one_hot, wk[:], per_tile(rk[:]), ALU.is_equal))

            def without(scores, one_hot):
                then(V.scalar_tensor_tensor(out=scores, in0=one_hot, scalar=-1e30, in1=scores,
                                            op0=ALU.mult, op1=ALU.add))

            dve.wait_ge(gate_done, 1)
            dve.wait_ge(cls_ready, 3)
            then(V.tensor_copy(sc[:, 0:J - 1, :], bank[0][:, 0:(J - 1) * E].rearrange("p (j e) -> p j e", e=E)))
            then(V.tensor_copy(sc[0:LAST, J - 1, :], bank[0][0:LAST, (J - 1) * E:J * E]))
            then(V.tensor_tensor(scb[:], sc[:], per_expert(gateb_sb[:]), ALU.add))
            first_best(scb[:], mx[:], pick[:, 0])
            without(scb[:], pick[:, 0])
            first_best(scb[:], mx[:], pick[:, 1])
            then(V.tensor_tensor(both[:], pick[:, 0], pick[:, 1], ALU.add))
            both_inc = V.tensor_copy(wk[:], both[:])
            both_inc.then_inc(both_ready, 1)
            first_best(sc[:], top[:, 0, :], pick_u[:])
            without(sc[:], pick_u[:])
            V.tensor_reduce(top[:, 1, :], sc[:], AX.X, ALU.max).then_inc(route, 1)
            dve.wait_ge(sg_e, 1)
            then(V.tensor_scalar(sg[:], sg[:], 1.0, None, ALU.add))
            then(V.reciprocal(sg[:], sg[:]))
            then(V.tensor_tensor(mx[:], sg[:, 0, :], sg[:, 1, :], ALU.add))
            then(V.reciprocal(mx[:], mx[:]))
            dve.wait_ge(ids_ready, 1)
            for k in range(2):
                last = V.tensor_tensor(xd[:, :, k, D + 1], sg[:, k, :], mx[:], ALU.mult)
            last.then_inc(weight_done, 1)
            dve.wait_ge(pref_done, 1)
            then(V.tensor_copy(cnt[:], bank[2][:, 0:J * E].rearrange("p (j e) -> p e j", e=E)))
            then(V.tensor_tensor_scan(inc[:].rearrange("p e j -> p (e j)"), cst[:, C_RESET:C_RESET + E * J],
                                      cnt[:].rearrange("p e j -> p (e j)"), 0.0, ALU.mult, ALU.add))
            then(V.tensor_tensor(exc[:], inc[:], cnt[:], ALU.subtract))
            then(V.tensor_tensor(exc[:], exc[:], cst[:, C_BASE:C_BASE + E].rearrange("p (e o) -> p e o", o=1)
                                 .broadcast_to([P, E, J]), ALU.add))
            then(V.tensor_tensor(place[:], bank[1][:, 0:J * E].rearrange("p (j e) -> p j e", e=E),
                                 exc[:].rearrange("p e j -> p j e"), ALU.add))
            then(V.tensor_tensor(prod[:], pick[:], place[:].rearrange("p (o j) e -> p o j e", o=1)
                                 .broadcast_to([P, 2, J, E]), ALU.mult))
            then(V.tensor_reduce(pos_f[:], prod[:], AX.X, ALU.add))
            V.tensor_copy(pos_i[:], pos_f[:]).then_inc(pos_done, 1)
            n_e = inc[:, :, J - 1]
            then(V.tensor_scalar(tn[:], n_e, float(P - 1), None, ALU.add))
            then(V.tensor_copy(ti[:, 0, :], tn[:]))
            then(V.tensor_scalar(ti[:, 1, :], ti[:, 0, :], 7, None, ALU.arith_shift_right))
            then(V.tensor_copy(tf[:], ti[:, 1, :]))
            then(V.tensor_tensor_scan(te[:], cst[:, C_ONE:C_ONE + E], tf[:], 0.0, ALU.mult, ALU.add))
            def tiles_of(ap):
                return ap.rearrange("p (o e) -> p o e", o=1).broadcast_to([P, TILES, E])
            iota = cst[:, C_IOTA:C_IOTA + TILES]
            then(V.tensor_tensor(ge[:], iota.rearrange("p (t o) -> p t o", o=1).broadcast_to([P, TILES, E]),
                                 tiles_of(te[:]), ALU.is_ge))
            then(V.tensor_reduce(t_e[:], ge[:], AX.X, ALU.add))
            then(V.tensor_tensor(gn[:], ge[:], tiles_of(tf[:]), ALU.mult))
            then(V.tensor_reduce(t_s[:], gn[:], AX.X, ALU.add))
            then(V.tensor_tensor(t_s[:], iota, t_s[:], ALU.subtract))
            then(V.tensor_scalar(t_r[:, 0, :], t_e[:], float(CAP), None, ALU.mult))
            then(V.scalar_tensor_tensor(out=t_r[:, 1, :], in0=t_s[:], scalar=float(P), in1=t_r[:, 0, :],
                                        op0=ALU.mult, op1=ALU.add))
            then(V.tensor_scalar(t_r[:, 1, :], t_r[:, 1, :], float(E * CAP), None, ALU.min))
            then(V.tensor_copy(tab_r[:], t_r[:, 1, :]))
            then(V.tensor_scalar(t_e[:], t_e[:], float(E - 1), None, ALU.min))
            then(V.tensor_copy(tab_e[:], t_e[:]))
            then(V.tensor_tensor(tn[:], n_e, cst[:, C_BASE:C_BASE + E], ALU.add))
            V.tensor_copy(tab_p[:], tn[:]).then_inc(tab_done, 1)

            for j in range(J):
                rows = P if j < J - 1 else LAST
                dve.wait_ge(xd_tr, j + 1)
                V.tensor_copy(xd[0:rows, j, :, 0:D],
                              bank[5 + j % 2][0:rows, 0:D].rearrange("p (o d) -> p o d", o=1)
                              .broadcast_to([rows, 2, D])).then_inc(xd_ready, 1)

            with dve.Fori(0, G) as i:
                g = dve.snap(i)
                for m in range(2):
                    dve.wait_ge(sh_act, 2 * g + m + 1)
                    if m == 0:
                        dve.wait_ge(sh_down, g)
                    V.tensor_tensor(sh_h[m][:], sh_s[m][:], bank[2 + m][:, 0:GN], ALU.mult).then_inc(sh_mul, 1)
                dve.wait_ge(sh_down, g + 1)
                V.tensor_tensor(h2T[:, bass.ds(g * GN, GN)], h2T[:, bass.ds(g * GN, GN)], bank[4][:, 0:GN], ALU.add
                                ).then_inc(sh_add, 1)

            def untransposed(t, q):
                dve.wait_ge(tx_done, t + 1)
                after(dve, up_done, t - 1)
                V.tensor_copy(xsT[q][:], bank[q][:, 0:P]).then_inc(xsT_done, 1)

            def gated(t, q):
                dve.wait_ge(silu_done, t + 1)
                after(dve, th_done, t - 1)
                V.tensor_tensor(hm[q][:], hs[q][:], bank[2 + q][:, HID:2 * HID], ALU.mult).then_inc(hm_done, 1)

            def tiles(n, last=False):
                for u in range(U):
                    t = U * n + u
                    if not (last and u == U - 1):
                        untransposed(t + 1, (u + 1) % 2)
                    gated(t, u % 2)

            untransposed(0, 0)
            tiles(0)
            with dve.Fori(1, TILES // U - 1) as n:
                tiles(dve.snap(n))
            tiles(TILES // U - 1, last=True)

            for c in range(J // YC):
                n_dma = 4 if c == J // YC - 1 else 2
                dve.wait_ge(y_loaded[c % 2], 16 * (2 * (c // 2) + n_dma))
                if c == 0:
                    dve.wait_ge(res_copied, J)
                if c < J // YC - 1:
                    parts = [(P, 0, YC)]
                else:
                    parts = [(P, 0, YC - 1), (LAST, YC - 1, YC)]
                for rows, a, b in parts:
                    last = V.tensor_tensor(yb[c % 2][0:rows, a:b, :], yb[c % 2][0:rows, a:b, :],
                                           res[0:rows, c * YC + a:c * YC + b, :], ALU.add)
                last.then_inc(fin_a, 1)
                dve.wait_ge(fin_a, c + 1)
                for rows, a, b in parts:
                    last = V.tensor_tensor(ya[c % 2][0:rows, a:b, :], ya[c % 2][0:rows, a:b, :],
                                           yb[c % 2][0:rows, a:b, :], ALU.add)
                last.then_inc(fin_done, 1)

        @block.tensor
        def _(pe):
            M, T = nc.tensor.matmul, nc.tensor.transpose

            def tokens(p, n):
                g = 2 * n + p
                pe.wait_ge(x_loaded[p], 32 * n + 32)
                after(pe, hpatch_done, g)
                for k in range(KB):
                    M(ps_tok[:, 0:P], wt[:, k, :], xp[p][:, k, :], start=(k == 0), stop=False)
                M(ps_tok[:, 0:P], wt_rest[:], xr[p][:], start=False, stop=True).then_inc(tok_done, 1)

            def mean_1(p, n):
                g = 2 * n + p
                pe.wait_ge(hpatch_done, g + 1)
                pe.wait_ge(txt_loaded[p], 16 * n + 16)
                after(pe, lv1_done, g)
                M(ps_ln1[:, 0:GN], mean_w, hT[p][:].rearrange("p b t -> p (b t)"), start=True, stop=True
                  ).then_inc(mean1, 1)

            def var_1(p, n):
                g = 2 * n + p
                pe.wait_ge(sq1_done, g + 1)
                M(ps_ln1[:, 0:GN], mean_w, sq1[:], start=True, stop=True).then_inc(var1, 1)

            def mean_2(p, n):
                g = 2 * n + p
                pe.wait_ge(h2_done, g + 1)
                after(pe, lv2_done, g)
                M(ps_ln2[:, 0:GN], mean_w, h2T[:, bass.ds(g * GN, GN)], start=True, stop=True).then_inc(mean2, 1)

            def var_2(p, n):
                g = 2 * n + p
                pe.wait_ge(sq2_done, g + 1)
                M(ps_ln2[:, 0:GN], mean_w, sq2[:], start=True, stop=True).then_inc(var2, 1)

            def project(p, g, k):
                at, rows, _ = PIECES[k]
                x = xT[p][:].rearrange("p b t -> p (b t)")[:, at:at + rows]
                if k == 0:
                    pe.wait_ge(xT_done, g + 1)
                if k < 2:
                    after(pe, qk_done[k + 2], g)
                    after(pe, v_done[k + 2], g)
                else:
                    pe.wait_ge(qk_done[k - 2], g + 1)
                    pe.wait_ge(v_done[k - 2], g + 1)
                M(ps_qkv[k % 2][0:rows, 0:2 * D], x, wqk_sb[:], start=True, stop=True)
                T(ps_qkv[k % 2][0:rows, 2 * D:3 * D], x, ident).then_inc(qkv_done[k], 1)

            def turn(g, j):
                after(pe, qq_done[1 - j], g + j)
                for k in (2 * j, 2 * j + 1):
                    at, rows = PIECES[k][0] - j * SEQ, PIECES[k][1]
                    pe.wait_ge(ft_done[k], g + 1)
                    T(ps_tr[:, at:at + rows], ft[k][0:rows, 0:D], ident[0:rows, 0:rows])
                    pe.wait_ge(rr_done[k], g + 1)
                    last = T(ps_tr[:, SEQ + at:SEQ + at + rows], rr[k][0:rows, 0:D], ident[0:rows, 0:rows])
                last.then_inc(qT_done[j], 1)

            def sums(g, j):
                after(pe, kvm_done[1 - j], g + j)
                for i, k in enumerate((2 * j, 2 * j + 1)):
                    rows = PIECES[k][1]
                    pe.wait_ge(v_done[k], g + 1)
                    M(ps_kv[:, 0:D], rr[k][0:rows, D:2 * D], vt[k][0:rows, :], start=(i == 0), stop=(i == 1))
                for i, k in enumerate((2 * j, 2 * j + 1)):
                    rows = PIECES[k][1]
                    last = M(ps_kv[:, D:D + 2], ft[k][0:rows, D:2 * D], ones[0:rows, 0:2], start=(i == 0), stop=(i == 1))
                last.then_inc(kv_done[j], 1)

            def attend(g, j):
                pe.wait_ge(kvm_done[j], g + 1)
                pe.wait_ge(qq_done[j], g + 1)
                after(pe, ot_done[1 - j], g + j)
                M(ps_od[:, 0:SEQ], kvm[j][:, 0, :], qq[j][:, 1, :], start=True, stop=True)
                M(ps_od[:, SEQ:2 * SEQ], kvm[j][:, 1, :], qq[j][:, 0, :], start=True, stop=True
                  ).then_inc(od_done[j], 1)

            def group(p, n, first=False, last=False):
                g = 2 * n + p
                before = (1 - p, n - 1 if p == 0 else n)
                behind = (1 - p, n if p == 0 else n + 1)
                for k in range(4):
                    project(p, g, k)
                if not first:
                    mean_2(*before)
                if not last:
                    tokens(*behind)
                turn(g, 0)
                sums(g, 0)
                if not first:
                    var_2(*before)
                if not last:
                    mean_1(*behind)
                turn(g, 1)
                sums(g, 1)
                attend(g, 0)
                if not last:
                    var_1(*behind)
                attend(g, 1)

            pe.wait_ge(s_wtok, 32)
            tokens(0, 0)
            pe.wait_ge(s_cst, 16)
            pe.wait_ge(s_small, 160)
            pe.wait_ge(cls_ready, 2)
            mean_1(0, 0)
            var_1(0, 0)
            group(0, 0, first=True)
            with pe.Fori(0, G // 2 - 1) as i:
                n = pe.snap(i)
                group(1, n)
                group(0, n + 1)
            group(1, G // 2 - 1, last=True)
            mean_2(1, G // 2 - 1)
            var_2(1, G // 2 - 1)

            pe.wait_ge(x2_done, G)
            for j in range(J):
                rows = P if j < J - 1 else LAST
                last = M(bank[0][0:rows, E * j:E * j + E], x2T[:, P * j:P * j + rows], gate_sb[:], start=True, stop=True)
            last.then_inc(gate_done, 1)

            def turn_row(j):
                rows = P if j < J - 1 else LAST
                after(pe, xd_ready, j - 1)
                T(bank[5 + j % 2][0:rows, 0:D], x2T[:, P * j:P * j + rows], ident).then_inc(xd_tr, 1)

            turn_row(0)
            turn_row(1)
            pe.wait_ge(both_ready, 1)
            full = (J - 1) * E
            flat = both[:].rearrange("p j e -> p (j e)")
            M(bank[1][:, 0:full], tri, flat[:, 0:full], start=True, stop=True)
            M(bank[1][:, full:J * E], tri[0:LAST, :], flat[0:LAST, full:J * E], start=True, stop=True)
            M(bank[2][:, 0:full], ones, flat[:, 0:full], start=True, stop=True)
            M(bank[2][:, full:J * E], ones[0:LAST, :], flat[0:LAST, full:J * E], start=True, stop=True
              ).then_inc(pref_done, 1)
            for j in range(2, J):
                turn_row(j)

            pe.wait_ge(s_wexp, 96)
            pe.wait_ge(pos_done, 1)
            with pe.Fori(0, G) as i:
                g = pe.snap(i)
                x = x2T[:, bass.ds(g * GN, GN)]
                pe.wait_ge(sh_mul, 2 * g)
                for m in range(2):
                    M(bank[2 + m][:, 0:GN], sw13[:, HID + P * m:HID + P * m + P], x, start=True, stop=True)
                    M(bank[m][:, 0:GN], sw13[:, P * m:P * m + P], x, start=True, stop=True).then_inc(sh_up, 1)
                pe.wait_ge(sh_add, g)
                for m in range(2):
                    pe.wait_ge(sh_mul, 2 * g + m + 1)
                    last = M(bank[4][:, 0:GN], sw2_sb[:, m, :], sh_h[m][:], start=(m == 0), stop=(m == 1))
                last.then_inc(sh_down, 1)
            pe.wait_ge(sh_add, G)
            for j in range(J):
                rows = P if j < J - 1 else LAST
                after(pe, res_copied, j - 1)
                T(bank[6 + j % 2][0:rows, 0:D], h2T[:, P * j:P * j + rows], ident).then_inc(res_tr, 1)

            pe.wait_ge(tab_done, 1)

            def load_expert(t):
                return pe.value_load(tab_e[0:1, bass.ds(t, 1)] if not isinstance(t, int) else tab_e[0:1, t:t + 1],
                                     min_val=0, max_val=E - 1)

            def transposed(t, q, u, n):
                pe.wait_ge(xs_loaded[u], 16 * n + 16)
                after(pe, xsT_done, t - 1)
                T(bank[q][:, 0:P], xs[u][:, 0:D], ident).then_inc(tx_done, 1)

            def up(t, q, e):
                pe.wait_ge(xsT_done, t + 1)
                after(pe, hm_done, t - 1)
                M(bank[2 + q][:, 0:2 * HID], xsT[q][:], w13[:].rearrange("p e h -> p (e h)")[:, bass.ds(e * (2 * HID), 2 * HID)],
                  start=True, stop=True).then_inc(up_done, 1)

            def hidden(t, q):
                pe.wait_ge(hm_done, t + 1)
                after(pe, hmT_done, t - 1)
                for m in range(2):
                    last = T(bank[4 + q][:, P * m:P * m + P], hm[q][:, P * m:P * m + P], ident)
                last.then_inc(th_done, 1)

            def down(t, q, e):
                pe.wait_ge(hmT_done, t + 1)
                after(pe, ys_done, t - 1)
                w = w2_sb[:].rearrange("p e k d -> p (e k d)")
                for m in range(2):
                    last = M(bank[6 + q][:, 0:D], hmT[q][:, m, :], w[:, bass.ds(e * (2 * D) + m * D, D)],
                             start=(m == 0), stop=(m == 1))
                last.then_inc(dn_done, 1)

            def tiles(n, first=False, last=False):
                for u in range(U):
                    t = U * n + u
                    up(t, u % 2, load_expert(t))
                    if not (last and u == U - 1):
                        transposed(t + 1, (u + 1) % 2, (u + 1) % U, n if u < U - 1 else n + 1)
                    if not (first and u < 1):
                        hidden(t - 1, (u - 1) % 2)
                    if not (first and u < 2):
                        down(t - 2, u % 2, load_expert(t - 2))

            pe.wait_ge(res_copied, J)
            transposed(0, 0, 0, 0)
            tiles(0, first=True)
            with pe.Fori(1, TILES // U - 1) as n:
                tiles(pe.snap(n))
            tiles(TILES // U - 1, last=True)
            hidden(TILES - 1, 1)
            down(TILES - 2, 0, load_expert(TILES - 2))
            down(TILES - 1, 1, load_expert(TILES - 1))


_OUT = (NTOK, D)


def kernel(x, txt, L0_tok_W, L0_tok_b, L0_tok_class_token, L0_tok_pos_embed, L0_attn_Wqk, L0_attn_bqk,
           L0_attn_lepe_w, L0_attn_lepe_b, L0_ffn_gate_w, L0_ffn_biases, L0_ffn_w1, L0_ffn_w3, L0_ffn_w2,
           L0_ffn_sw1, L0_ffn_sw3, L0_ffn_sw2):
    import concourse.bacc as bacc
    from concourse.bass_utils import run_bass_kernel_spmd

    con = np.ascontiguousarray
    patches = x.reshape(G, 2, CH, GRID, PATCH, GRID, PATCH).transpose(0, 2, 4, 6, 1, 3, 5)
    arrays = {
        "patches": con(patches).reshape(G * IN_D, 2 * NP_),
        "txt": con(txt.transpose(2, 0, 1)).reshape(D, B * NT),
        "w_tok": con(L0_tok_W.transpose(1, 0)),
        "b_tok": L0_tok_b.reshape(D, 1),
        "cls": L0_tok_class_token.reshape(D, 1),
        "pos": con(L0_tok_pos_embed.transpose(1, 0)),
        "wqk": con(L0_attn_Wqk),
        "bqk": L0_attn_bqk.reshape(1, 2 * D),
        "lepe_w": L0_attn_lepe_w.reshape(D, 3),
        "lepe_b": L0_attn_lepe_b.reshape(D, 1),
        "gate_w": con(L0_ffn_gate_w.transpose(1, 0)),
        "gate_b": L0_ffn_biases.reshape(1, E),
        "w1": con(L0_ffn_w1), "w3": con(L0_ffn_w3), "w2": con(L0_ffn_w2),
        "sw1": con(L0_ffn_sw1), "sw3": con(L0_ffn_sw3), "sw2": con(L0_ffn_sw2),
        "consts": constants(),
        "dests": destinations(),
    }
    arrays = {f"in_{k}": np.asarray(v) for k, v in arrays.items()}
    nc = bacc.Bacc("TRN2", target_bir_lowering=False, num_devices=1)
    args = [nc.dram_tensor(k, a.shape, mybir.dt.from_np(a.dtype), kind="ExternalInput").ap()
            for k, a in arrays.items()]
    args.append(nc.dram_tensor("out_tokens", _OUT, F32, kind="ExternalOutput").ap())
    build(nc, *args)
    r = run_bass_kernel_spmd(nc, [arrays], core_ids=[0])
    return np.asarray(r.results[0]["out_tokens"]).reshape(B, SEQ, D)
```

```python
import numpy as np
import concourse.bass as bass
from concourse import mybir
from contextlib import ExitStack

F32 = mybir.dt.float32
I32 = mybir.dt.int32
U32 = mybir.dt.uint32
ALU = mybir.AluOpType
ACT = mybir.ActivationFunctionType
AX = mybir.AxisListType

P = 128
B, CH, IMG, GRID = 16, 3, 224, 8
PATCH = IMG // GRID
IN_D = CH * PATCH * PATCH
KB = IN_D // P
KR = IN_D - KB * P
D = 128
NP_, NT = GRID * GRID, 128
SEQ = 1 + NP_ + NT
NTOK = B * SEQ
H, HD = 8, 16
G = B // 2
GN = 2 * SEQ
LN_EPS, Z_EPS = 1e-5, 1e-6
E, HID = 8, 256
PIECES = [(0, 1 + NP_, 0), (1 + NP_, NT, 1), (SEQ, 1 + NP_, 0), (SEQ + 1 + NP_, NT, 1)]
J = -(-NTOK // P)
LAST = NTOK - (J - 1) * P
CAP = NTOK + P
TILES = (2 * NTOK - E) // P + E
DEAD = TILES - (2 * NTOK) // P
ROW = D + 2
BIG = 1 << 20
U = 8
SLOTS = 2
assert TILES % U == 0 and U % SLOTS == 0 and G % 2 == 0

C_ID, C_MEAN, C_TRI, C_ONE, C_MASK = 0, P, 2 * P, 3 * P, 4 * P
C_COS, C_SIN = 5 * P, 5 * P + 4 * P
C_RANK, C_TILE, C_RESET = 13 * P, 13 * P + 8, 14 * P
C_BASE = C_RESET + E * J
C_IOTA = C_BASE + E
NCONST = C_IOTA + TILES


def constants():
    c = np.zeros((P, NCONST), np.float32)
    c[:, C_ID:C_ID + P] = np.eye(P)
    c[:, C_MEAN:C_MEAN + P] = 1.0 / D
    c[:, C_TRI:C_TRI + P] = np.triu(np.ones((P, P)), 1)
    c[:, C_ONE:C_ONE + P] = 1.0
    head = np.arange(P) // HD
    c[:, C_MASK:C_MASK + P] = (head[:, None] == head[None, :]) / SEQ
    inv = 1.0 / 10000.0 ** (np.arange(0, HD, 2, dtype=np.float32) / HD)
    freq = np.outer(np.arange(SEQ, dtype=np.float32), inv).astype(np.float32)
    cos, sin = np.cos(freq), np.sin(freq)
    for half, (start, rows) in enumerate(((0, 1 + NP_), (1 + NP_, NT))):
        at = slice(start, start + rows)
        c[:rows, C_COS + 256 * half:C_COS + 256 * half + 256] = np.tile(np.concatenate([cos[at], cos[at]], 1), (1, 16))
        c[:rows, C_SIN + 256 * half:C_SIN + 256 * half + 256] = np.tile(np.concatenate([-sin[at], sin[at]], 1), (1, 16))
    c[:, C_RANK:C_RANK + E] = np.arange(E, 0, -1)
    reset = np.ones((E, J))
    reset[:, 0] = 0
    c[:, C_RESET:C_RESET + E * J] = reset.reshape(-1)
    c[:, C_BASE:C_BASE + E] = np.arange(E) * CAP
    c[:, C_IOTA:C_IOTA + TILES] = np.arange(TILES)
    return c


def destinations():
    flat = np.arange(J)[None, :, None] * P + np.arange(P)[:, None, None]
    ids = flat + np.arange(2)[None, None, :] * NTOK
    return np.concatenate([ids.reshape(P, 2 * J), np.full((P, 1), BIG)], 1).astype(np.int32)


def build(nc, patches, txt, w_tok, b_tok, cls, pos, wqk, bqk, lepe_w, lepe_b, gate_w, gate_b,
          w1, w3, w2, sw1, sw3, sw2, consts, dests, out):
    xs_dram = nc.dram_tensor("xs_dram", [E * CAP + DEAD * P, ROW], F32).ap()
    y_dram = nc.dram_tensor("y_dram", [2 * NTOK, D], F32).ap()
    ctx = ExitStack()
    with ctx:
        def sb(name, shape, dt=F32):
            return ctx.enter_context(nc.sbuf_tensor(name, shape, dt))

        def pb(name):
            return ctx.enter_context(nc.psum_tensor(name, [P, 512], F32))

        def sem(name):
            return ctx.enter_context(nc.semaphore(name))

        def sems(name, n):
            return [sem(f"{name}{i}") for i in range(n)]

        cst = sb("cst", [P, NCONST])
        ident, mean_w = cst[:, C_ID:C_ID + P], cst[:, C_MEAN:C_MEAN + P]
        tri, ones, mask = cst[:, C_TRI:C_TRI + P], cst[:, C_ONE:C_ONE + P], cst[:, C_MASK:C_MASK + P]
        dest_sb = sb("dest_sb", [P, 2 * J + 1], I32)
        wt = sb("wt", [P, KB, D])
        wt_rest = sb("wt_rest", [KR, D])
        cols = sb("cols", [P, 8])
        pos_sb = sb("pos_sb", [P, 1 + NP_])
        wqk_sb = sb("wqk_sb", [P, 2 * D])
        bqk_sb = sb("bqk_sb", [P, 2 * D])
        gate_sb = sb("gate_sb", [P, E])
        gateb_sb = sb("gateb_sb", [P, E])
        w13 = sb("w13", [P, E, 2 * HID])
        w2_sb = sb("w2_sb", [P, E, 2, D])
        sw13 = sb("sw13", [P, 2 * HID])
        sw2_sb = sb("sw2_sb", [P, 2, D])

        xp = [sb(f"xp{i}", [P, KB, P]) for i in range(2)]
        xr = [sb(f"xr{i}", [KR, P]) for i in range(2)]
        hT = [sb(f"hT{i}", [P, 2, SEQ]) for i in range(2)]
        dev1, sq1, lv1, rs1 = (sb(n, [P, GN]) for n in ("dev1", "sq1", "lv1", "rs1"))
        dev2, sq2, lv2, rs2 = (sb(n, [P, GN]) for n in ("dev2", "sq2", "lv2", "rs2"))
        xT = [sb(f"xT{i}", [P, 2, SEQ]) for i in range(2)]
        att = sb("att", [P, 5, 4, 2 * D])
        qk, ex, rl, ft, rr = ([att[:, i, k, :] for k in range(4)] for i in range(5))
        cc, ss = ex, rl
        vt = [sb(f"vt{k}", [P, D]) for k in range(4)]
        qq = [sb(f"qq{j}", [P, 2, SEQ]) for j in range(2)]
        kvm = [sb(f"kvm{j}", [P, 2, D]) for j in range(2)]
        zt = [sb(f"zt{j}", [P, SEQ]) for j in range(2)]
        zr = [sb(f"zr{j}", [P, SEQ]) for j in range(2)]
        ot = sb("ot", [P, 2, SEQ])
        hl = [sb(f"hl{i}", [P, 2, SEQ]) for i in range(2)]
        h2T = sb("h2T", [P, NTOK])
        x2T = sb("x2T", [P, NTOK])

        bank = [pb(f"bank{i}") for i in range(8)]
        ps_ln1, ps_ln2, ps_tok = bank[0], bank[1], bank[2]
        ps_qkv, ps_tr, ps_kv, ps_od = bank[3:5], bank[5], bank[6], bank[7]

        sc = sb("sc", [P, J, E])
        scb = sb("scb", [P, J, E])
        eq = sb("eq", [P, J, E])
        wk = sb("wk", [P, J, E])
        pick = sb("pick", [P, 2, J, E])
        pick_u = sb("pick_u", [P, J, E])
        top = sb("top", [P, 2, J])
        mx = sb("mx", [P, J])
        rk = sb("rk", [P, J])
        sg = sb("sg", [P, 2, J])
        both = sb("both", [P, J, E])
        cnt = sb("cnt", [P, E, J])
        inc = sb("inc", [P, E, J])
        exc = sb("exc", [P, E, J])
        place = sb("place", [P, J, E])
        prod = sb("prod", [P, 2, J, E])
        pos_f = sb("pos_f", [P, 2, J])
        pos_i = sb("pos_i", [P, 2, J], I32)
        tn = sb("tn", [P, E])
        ti = sb("ti", [P, 2, E], I32)
        tf = sb("tf", [P, E])
        te = sb("te", [P, E])
        ge = sb("ge", [P, TILES, E])
        gn = sb("gn", [P, TILES, E])
        t_e = sb("t_e", [P, TILES])
        t_s = sb("t_s", [P, TILES])
        t_r = sb("t_r", [P, 2, TILES])
        tab_e = sb("tab_e", [P, TILES], I32)
        tab_r = sb("tab_r", [P, TILES], I32)
        tab_p = sb("tab_p", [P, E], I32)
        xd = sb("xd", [P, J, 2, ROW])
        pad = sb("pad", [P, ROW])

        xs = [sb(f"xs{u}", [P, ROW]) for u in range(U)]
        xsT = [sb(f"xsT{u}", [P, P]) for u in range(2)]
        hs = [sb(f"hs{u}", [P, HID]) for u in range(2)]
        hm = [sb(f"hm{u}", [P, HID]) for u in range(2)]
        hmT = [sb(f"hmT{u}", [P, 2, P]) for u in range(2)]
        ys = [sb(f"ys{u}", [P, D]) for u in range(U)]
        sh_s = [dev1, sq1]
        sh_h = [dev2, sq2]
        YC = 5
        ya = [xp[i][:, 0:YC, :] for i in range(2)]
        yb = [xp[i][:, YC:2 * YC, :] for i in range(2)]
        res = att[:].rearrange("p a k c -> p (a k c)")[:, 0:J * D].rearrange("p (j d) -> p j d", d=D)

        s_cst, s_wtok, s_small, s_wexp = sem("s_cst"), sem("s_wtok"), sem("s_small"), sem("s_wexp")
        x_loaded, txt_loaded = sems("x_loaded", 2), sems("txt_loaded", 2)
        cls_ready = sem("cls_ready")
        tok_done, hpatch_done = sem("tok_done"), sem("hpatch_done")
        mean1, dev1_done, sq1_done, var1, lv1_done, rs1_done = (
            sem(n) for n in ("mean1", "dev1_done", "sq1_done", "var1", "lv1_done", "rs1_done"))
        mean2, dev2_done, sq2_done, var2, lv2_done, rs2_done = (
            sem(n) for n in ("mean2", "dev2_done", "sq2_done", "var2", "lv2_done", "rs2_done"))
        xT_done, x2_done = sem("xT_done"), sem("x2_done")
        qkv_done, qk_done, v_done = sems("qkv_done", 4), sems("qk_done", 4), sems("v_done", 4)
        ex_done, rl_done, ft_done = sems("ex_done", 4), sems("rl_done", 4), sems("ft_done", 4)
        cc_done, ss_done, rr_done = sems("cc_done", 4), sems("ss_done", 4), sems("rr_done", 4)
        qT_done, qq_done = sems("qT_done", 2), sems("qq_done", 2)
        kv_done, kvm_done, od_done = sems("kv_done", 2), sems("kvm_done", 2), sems("od_done", 2)
        zt_done, zr_done, ot_done = sems("zt_done", 2), sems("zr_done", 2), sems("ot_done", 2)
        lc_done, lh_done, tap_done, hl_done, h2_done = (
            sem(n) for n in ("lc_done", "lh_done", "tap_done", "hl_done", "h2_done"))
        ids_ready, pad_ready = sem("ids_ready"), sem("pad_ready")
        gate_done, sc_done, route, sg_e, both_ready, pref_done, pos_done = (
            sem(n) for n in ("gate_done", "sc_done", "route", "sg_e", "both_ready", "pref_done", "pos_done"))
        weight_done, tab_done, route_chain = sem("weight_done"), sem("tab_done"), sem("route_chain")
        xd_tr, xd_copied = sem("xd_tr"), sem("xd_copied")
        xd_ready = sem("xd_ready")
        scattered, padded = sem("scattered"), sem("padded")
        sh_up, sh_act, sh_mul, sh_down, sh_add = (
            sem(n) for n in ("sh_up", "sh_act", "sh_mul", "sh_down", "sh_add"))
        res_tr, res_copied = sem("res_tr"), sem("res_copied")
        xs_loaded = sems("xs_loaded", U)
        tx_done, xsT_done, up_done, silu_done, hm_done, th_done, hmT_done, dn_done, ys_done = (
            sems(n, SLOTS) for n in ("tx_done", "xsT_done", "up_done", "silu_done", "hm_done", "th_done",
                                 "hmT_done", "dn_done", "ys_done"))
        y_sent = sems("y_sent", U)
        y_loaded, fin_a, fin_done, out_sent = sems("y_loaded", 2), sem("fin_a"), sem("fin_done"), sems("out_sent", 2)

        block = ctx.enter_context(nc.Block())

        def after(eng, s, value):
            if not isinstance(value, int) or value > 0:
                eng.wait_ge(s, value)

        def slot(u, back):
            return (u - back) % SLOTS

        def turns(n, u, back):
            k = (u - back) // SLOTS + 1
            return n * (U // SLOTS) + k if isinstance(n, int) else n[k]

        def exists(n, u, back):
            return not isinstance(n, int) or 0 <= U * n + u - back < TILES

        def expert_steps(eng, step, depth):
            for u in range(U):
                step(0, u)
            regs = {k: eng.alloc_register(f"turn{k + 2}") for k in range(-2, U // SLOTS + 1)}
            for k in regs:
                eng.reg_mov(regs[k], U // SLOTS + k)
            with eng.Fori(1, TILES // U):
                for u in range(U):
                    step(regs, u)
                for k in regs:
                    eng.reg_add(regs[k], regs[k], U // SLOTS)
            for u in range(depth):
                step(TILES // U, u)

        def two(eng, body):
            body(0, 0)
            with eng.Fori(0, G // 2 - 1) as i:
                n = eng.snap(i)
                body(1, n)
                body(0, n + 1)
            body(1, G // 2 - 1)

        @block.sync
        def _(sp):
            def load_group(p, n):
                g = 2 * n + p
                at, rest, tokens, old = [
                    v if isinstance(v, int) else sp.snap(v)
                    for v in (g * IN_D, g * IN_D + KB * P, g * 2 * NT, g - 1)]
                after(sp, tok_done, old)
                sp.dma_start(xp[p][:], patches[bass.ds(at, KB * P), :].rearrange(
                    "(q k) t -> q k t", k=KB)).then_inc(x_loaded[p], 16)
                sp.dma_start(xr[p][:], patches[bass.ds(rest, KR), :]).then_inc(x_loaded[p], 16)
                after(sp, h2_done, old)
                sp.dma_start(hT[p][:, :, 1 + NP_:SEQ], txt[:, bass.ds(tokens, 2 * NT)].rearrange(
                    "c (b t) -> c b t", b=2)).then_inc(txt_loaded[p], 16)

            sp.dma_start(wt[:], w_tok[0:KB * P, :].rearrange("(q k) h -> q k h", k=KB)).then_inc(s_wtok, 16)
            sp.dma_start(wt_rest[:], w_tok[KB * P:IN_D, :]).then_inc(s_wtok, 16)
            two(sp, load_group)

            sp.wait_ge(pad_ready, 2)
            sp.dma_start(xs_dram[E * CAP:, :].rearrange("(k q) r -> q k r", q=P),
                         pad[:].rearrange("p (o r) -> p o r", o=1).broadcast_to([P, DEAD, ROW])
                         ).then_inc(padded, 16)
            sp.wait_ge(tab_done, 1)
            for e in range(E):
                row = sp.value_load(tab_p[0:1, e:e + 1], min_val=0, max_val=E * CAP - P)
                sp.dma_start(xs_dram[bass.ds(row, P), :], pad[:]).then_inc(padded, 16)

            sp.wait_ge(scattered, 16 * 2 * J)
            sp.wait_ge(padded, 16 * (E + 1))

            sent_reg = sp.alloc_register("sent")

            def load_tiles(n, sent):
                for u in range(U):
                    row = sp.value_load(tab_r[0:1, bass.ds(U * n + u, 1)], min_val=0, max_val=E * CAP)
                    after(sp, y_sent[u], sent)
                    sp.dma_start(xs[u][:], xs_dram[bass.ds(row, P), :]).then_inc(xs_loaded[u], 16)

            load_tiles(0, 0)
            sp.reg_mov(sent_reg, 0)
            with sp.Fori(1, TILES // U) as n:
                sp.reg_add(sent_reg, sent_reg, 16)
                load_tiles(sp.snap(n), sent_reg)

            for u in range(U):
                sp.wait_ge(y_sent[u], 16 * (TILES // U))
            for c in range(J // YC):
                rows = YC * P if c < J // YC - 1 else (YC - 1) * P
                after(sp, out_sent[c % 2], (c // 2) * 16)
                for k, y in enumerate((ya, yb)):
                    at = k * NTOK + c * YC * P
                    sp.dma_start(y[c % 2][:, 0:rows // P, :], y_dram[at:at + rows, :].rearrange(
                        "(j q) d -> q j d", q=P)).then_inc(y_loaded[c % 2], 16)
                    if rows < YC * P:
                        sp.dma_start(y[c % 2][0:LAST, YC - 1, :], y_dram[at + rows:at + rows + LAST, :]
                                     ).then_inc(y_loaded[c % 2], 16)

        @block.scalar
        def _(act):
            A = nc.scalar.activation
            act.dma_start(cst[:], consts[:, :]).then_inc(s_cst, 16)
            act.dma_start(cols[:, 0:1], b_tok[:, :]).then_inc(s_small, 16)
            act.dma_start(cols[:, 1:2], cls[:, :]).then_inc(s_small, 16)
            act.dma_start(cols[:, 2:3], lepe_b[:, :]).then_inc(s_small, 16)
            act.dma_start(cols[:, 3:6], lepe_w[:, :]).then_inc(s_small, 16)
            act.dma_start(pos_sb[:], pos[:, :]).then_inc(s_small, 16)
            act.dma_start(wqk_sb[:], wqk[:, :]).then_inc(s_small, 16)
            act.dma_start(bqk_sb[:], bqk[:, :].broadcast_to([P, 2 * D])).then_inc(s_small, 16)
            act.dma_start(gate_sb[:], gate_w[:, :]).then_inc(s_small, 16)
            act.dma_start(gateb_sb[:], gate_b[:, :].broadcast_to([P, E])).then_inc(s_small, 16)
            act.dma_start(dest_sb[:], dests[:, :]).then_inc(s_small, 16)

            def square1(g):
                act.wait_ge(dev1_done, g + 1)
                A(sq1[:], dev1[:], ACT.Square).then_inc(sq1_done, 1)

            def rstd1(g):
                act.wait_ge(var1, g + 1)
                A(lv1[:], ps_ln1[:, 0:GN], ACT.Ln, bias=LN_EPS).then_inc(lv1_done, 1)
                act.wait_ge(lv1_done, g + 1)
                A(rs1[:], lv1[:], ACT.Exp, scale=-0.5).then_inc(rs1_done, 1)

            def square2(g):
                act.wait_ge(dev2_done, g + 1)
                A(sq2[:], dev2[:], ACT.Square).then_inc(sq2_done, 1)

            def rstd2(g):
                act.wait_ge(var2, g + 1)
                A(lv2[:], ps_ln2[:, 0:GN], ACT.Ln, bias=LN_EPS).then_inc(lv2_done, 1)
                act.wait_ge(lv2_done, g + 1)
                A(rs2[:], lv2[:], ACT.Exp, scale=-0.5).then_inc(rs2_done, 1)

            def piece(g, k):
                n = PIECES[k][1]
                act.wait_ge(qk_done[k], g + 1)
                after(act, kv_done[k // 2], g)
                nc.scalar.copy(vt[k][0:n, :], ps_qkv[k % 2][0:n, 2 * D:3 * D]).then_inc(v_done[k], 1)
                A(ex[k][0:n, :], qk[k][0:n, :], ACT.Exp).then_inc(ex_done[k], 1)
                A(rl[k][0:n, :], qk[k][0:n, :], ACT.Relu).then_inc(rl_done[k], 1)

            def queries(g, j):
                act.wait_ge(qT_done[j], g + 1)
                after(act, od_done[j], g)
                nc.scalar.copy(qq[j][:], ps_tr[:, 0:GN]).then_inc(qq_done[j], 1)

            def group(p, n, first=False, last=False):
                g = 2 * n + p
                piece(g, 0)
                after(act, h2_done, g - 1)
                act.wait_ge(xT_done, g + 1)
                A(hl[p][:], xT[p][:], ACT.Identity, bias=cols[:, 2:3], scale=cols[:, 4:5]).then_inc(lc_done, 1)
                piece(g, 1)
                piece(g, 2)
                if not first:
                    square2(g - 1)
                piece(g, 3)
                if not first:
                    rstd2(g - 1)
                queries(g, 0)
                if not last:
                    square1(g + 1)
                queries(g, 1)
                if not last:
                    rstd1(g + 1)

            act.wait_ge(s_small, 160)
            square1(0)
            rstd1(0)
            act.dma_start(sw13[:, 0:HID], sw1[:, :]).then_inc(s_wexp, 16)
            act.dma_start(sw13[:, HID:2 * HID], sw3[:, :]).then_inc(s_wexp, 16)
            act.dma_start(sw2_sb[:], sw2.rearrange("(k q) d -> q k d", q=P)).then_inc(s_wexp, 16)
            act.dma_start(w13[:, :, 0:HID], w1.rearrange("e d h -> d e h")).then_inc(s_wexp, 16)
            act.dma_start(w13[:, :, HID:2 * HID], w3.rearrange("e d h -> d e h")).then_inc(s_wexp, 16)
            act.dma_start(w2_sb[:], w2.rearrange("e (k q) d -> q e k d", q=P)).then_inc(s_wexp, 16)
            group(0, 0, first=True)
            with act.Fori(0, G // 2 - 1) as i:
                n = act.snap(i)
                group(1, n)
                group(0, n + 1)
            group(1, G // 2 - 1, last=True)
            square2(G - 1)
            rstd2(G - 1)

            act.wait_ge(route, 1)
            A(sg[:], top[:], ACT.Exp, scale=-1.0).then_inc(sg_e, 1)

            with act.Fori(0, G) as i:
                g = act.snap(i)
                for m in range(2):
                    act.wait_ge(sh_up, 2 * g + m + 1)
                    act.wait_ge(sh_mul, 2 * g + m)
                    A(sh_s[m][:], bank[m][:, 0:GN], ACT.Silu).then_inc(sh_act, 1)
            for j in range(J):
                rows = P if j < J - 1 else LAST
                act.wait_ge(res_tr, j + 1)
                nc.scalar.copy(res[0:rows, j, :], bank[6 + j % 2][0:rows, 0:D]).then_inc(res_copied, 1)

            sent_reg = act.alloc_register("sent")
            act.reg_mov(sent_reg, 0)

            def gate(n, u):
                at, q = slot(u, 0), u % 2
                act.wait_ge(up_done[at], turns(n, u, 0))
                after(act, hm_done[slot(u, 2)], turns(n, u, 2))
                A(hs[q][:], bank[2 + q][:, 0:HID], ACT.Silu).then_inc(silu_done[at], 1)

            def turned(n, u):
                at, q = slot(u, 1), (u - 1) % 2
                act.wait_ge(th_done[at], turns(n, u, 1))
                after(act, dn_done[slot(u, 3)], turns(n, u, 3))
                nc.scalar.copy(hmT[q][:], bank[4 + q][:, 0:HID]).then_inc(hmT_done[at], 1)

            def result(n, u):
                at, q, buf = slot(u, 2), u % 2, (u - 2) % U
                act.wait_ge(dn_done[at], turns(n, u, 2))
                if isinstance(n, int):
                    after(act, y_sent[buf], 16 * (n - 1 if u < 2 else n))
                else:
                    if buf == 0:
                        act.reg_add(sent_reg, sent_reg, 16)
                    act.wait_ge(y_sent[buf], sent_reg)
                A(ys[buf][:], bank[6 + q][:, 0:D], ACT.Copy, scale=xs[buf][:, D + 1:D + 2]).then_inc(ys_done[at], 1)

            def act_step(n, u):
                if exists(n, u, 1):
                    turned(n, u)
                if exists(n, u, 0):
                    gate(n, u)
                if exists(n, u, 2):
                    result(n, u)

            expert_steps(act, act_step, 2)

            for c in range(J // YC):
                act.wait_ge(fin_done, c + 1)
                rows = YC * P if c < J // YC - 1 else (YC - 1) * P
                at = c * YC * P
                act.dma_start(out[at:at + rows, :].rearrange("(j q) d -> q j d", q=P),
                              ya[c % 2][:, 0:rows // P, :]).then_inc(out_sent[c % 2], 16)
                if rows < YC * P:
                    act.dma_start(out[at + rows:NTOK, :], ya[c % 2][0:LAST, YC - 1, :]
                                  ).then_inc(out_sent[c % 2], 16)
            n_even, n_odd = (J // YC + 1) // 2, (J // YC) // 2
            act.wait_ge(out_sent[0], 16 * (n_even + ((J // YC) % 2)))
            act.wait_ge(out_sent[1], 16 * (n_odd + 1 - ((J // YC) % 2)))

        @block.gpsimd
        def _(pool):
            pool.wait_ge(s_cst, 16)
            pool.wait_ge(s_small, 160)
            nc.gpsimd.memset(pad[:], 0.0).then_inc(pad_ready, 1)
            pool.wait_ge(pad_ready, 1)
            nc.gpsimd.tensor_copy(pad[:, D:D + 1].bitcast(I32), dest_sb[:, 2 * J:2 * J + 1]).then_inc(pad_ready, 1)
            nc.gpsimd.tensor_copy(xd[:, :, :, D:D + 1].bitcast(I32),
                                  dest_sb[:, 0:2 * J].rearrange("p (j k o) -> p j k o", k=2, o=1)
                                  ).then_inc(ids_ready, 1)

            def group(p, n):
                g = 2 * n + p
                for k in range(4):
                    rows, half = PIECES[k][1], PIECES[k][2]
                    pool.wait_ge(ft_done[k], g + 1)
                    after(pool, rr_done[k], g)
                    sin = cst[0:rows, C_SIN + 256 * half:C_SIN + 256 * half + 256]
                    nc.gpsimd.tensor_tensor(
                        ss[k][0:rows, :].rearrange("p (h t e) -> p h t e", t=2, e=8),
                        ft[k][0:rows, :].rearrange("p (h t e) -> p h t e", t=2, e=8)[:, :, ::-1, :],
                        sin.rearrange("p (h t e) -> p h t e", t=2, e=8), ALU.mult).then_inc(ss_done[k], 1)
                    if k == 0:
                        pool.wait_ge(lc_done, g + 1)
                        nc.gpsimd.tensor_tensor(hl[p][:], hl[p][:], hT[p][:], ALU.add).then_inc(lh_done, 1)

            two(pool, group)

            for j in range(J):
                rows = P if j < J - 1 else LAST
                pool.wait_ge(xd_ready, j + 1)
                if j == 0:
                    pool.wait_ge(pos_done, 1)
                    pool.wait_ge(weight_done, 1)
                for k in range(2):
                    nc.gpsimd.indirect_dma_start(
                        out=xs_dram[:, :], out_offset=bass.IndirectOffsetOnAxis(ap=pos_i[0:rows, k, j:j + 1], axis=0),
                        in_=xd[0:rows, j, k, :], in_offset=None).then_inc(scattered, 16)

            bound_reg = pool.alloc_register("bound")
            pool.reg_mov(bound_reg, 2 * NTOK - 1)
            bound = pool.snap(bound_reg)
            count = [pool.alloc_register(f"count{i}") for i in range(SLOTS)]
            for c in count:
                pool.reg_mov(c, 1)

            with pool.Fori(0, TILES // U):
                for u in range(U):
                    pool.wait_ge(ys_done[u % SLOTS], count[u % SLOTS])
                    pool.reg_add(count[u % SLOTS], count[u % SLOTS], 1)
                    nc.gpsimd.indirect_dma_start(
                        out=y_dram[:, :],
                        out_offset=bass.IndirectOffsetOnAxis(ap=xs[u][:, D:D + 1].bitcast(I32), axis=0),
                        in_=ys[u][:], in_offset=None, bounds_check=bound, oob_is_err=False).then_inc(y_sent[u], 16)

        @block.vector
        def _(dve):
            V = nc.vector

            def patch(p, n):
                g = 2 * n + p
                dve.wait_ge(tok_done, g + 1)
                after(dve, lh_done, g - 1)
                V.scalar_tensor_tensor(
                    out=hT[p][:, :, 1:1 + NP_], in0=ps_tok[:, 0:P].rearrange("p (b t) -> p b t", b=2),
                    scalar=cols[:, 0:1],
                    in1=pos_sb[:, 1:1 + NP_].rearrange("p (o t) -> p o t", o=1).broadcast_to([P, 2, NP_]),
                    op0=ALU.add, op1=ALU.mult).then_inc(hpatch_done, 1)

            def center1(p, n):
                g = 2 * n + p
                dve.wait_ge(mean1, g + 1)
                V.tensor_tensor(dev1[:].rearrange("p (b t) -> p b t", b=2), hT[p][:],
                                ps_ln1[:, 0:GN].rearrange("p (b t) -> p b t", b=2), ALU.subtract
                                ).then_inc(dev1_done, 1)

            def norm1(p, n):
                g = 2 * n + p
                dve.wait_ge(rs1_done, g + 1)
                after(dve, qkv_done[3], g - 1)
                V.tensor_tensor(xT[p][:].rearrange("p b t -> p (b t)"), dev1[:], rs1[:], ALU.mult).then_inc(xT_done, 1)

            def center2(p, n):
                g = 2 * n + p
                dve.wait_ge(mean2, g + 1)
                V.tensor_tensor(dev2[:], h2T[:, bass.ds(g * GN, GN)], ps_ln2[:, 0:GN], ALU.subtract
                                ).then_inc(dev2_done, 1)

            def norm2(p, n):
                g = 2 * n + p
                dve.wait_ge(rs2_done, g + 1)
                V.tensor_tensor(x2T[:, bass.ds(g * GN, GN)], dev2[:], rs2[:], ALU.mult).then_inc(x2_done, 1)

            def bias(g, k):
                n = PIECES[k][1]
                dve.wait_ge(qkv_done[k], g + 1)
                V.tensor_tensor(qk[k][0:n, :], ps_qkv[k % 2][0:n, 0:2 * D], bqk_sb[0:n, :], ALU.add
                                ).then_inc(qk_done[k], 1)

            def elu(g, k):
                n = PIECES[k][1]
                dve.wait_ge(ex_done[k], g + 1)
                dve.wait_ge(rl_done[k], g + 1)
                after(dve, kv_done[k // 2], g)
                after(dve, ss_done[k], g)
                V.scalar_tensor_tensor(out=ft[k][0:n, :], in0=ex[k][0:n, :], scalar=1.0, in1=rl[k][0:n, :],
                                       op0=ALU.min, op1=ALU.add).then_inc(ft_done[k], 1)

            def cosine(g, k):
                n, half = PIECES[k][1], PIECES[k][2]
                dve.wait_ge(ft_done[k], g + 1)
                V.tensor_tensor(cc[k][0:n, :], ft[k][0:n, :], cst[0:n, C_COS + 256 * half:C_COS + 256 * half + 256],
                                ALU.mult).then_inc(cc_done[k], 1)

            def rotated(g, k):
                n = PIECES[k][1]
                dve.wait_ge(cc_done[k], g + 1)
                dve.wait_ge(ss_done[k], g + 1)
                V.tensor_tensor(rr[k][0:n, :], cc[k][0:n, :], ss[k][0:n, :], ALU.add).then_inc(rr_done[k], 1)

            def heads(g, j):
                dve.wait_ge(kv_done[j], g + 1)
                after(dve, od_done[j], g)
                V.tensor_tensor(kvm[j][:, 0, :], ps_kv[:, 0:D], mask, ALU.mult)
                V.tensor_scalar(kvm[j][:, 1, :], mask, ps_kv[:, D:D + 1], None, ALU.mult).then_inc(kvm_done[j], 1)

            def attended(g, j):
                dve.wait_ge(od_done[j], g + 1)
                V.tensor_scalar(zt[j][:], ps_od[:, SEQ:2 * SEQ], Z_EPS, None, ALU.add).then_inc(zt_done[j], 1)
                dve.wait_ge(zt_done[j], g + 1)
                V.reciprocal(zr[j][:], zt[j][:]).then_inc(zr_done[j], 1)
                dve.wait_ge(zr_done[j], g + 1)
                V.tensor_tensor(ot[:, j, :], ps_od[:, 0:SEQ], zr[j][:], ALU.mult).then_inc(ot_done[j], 1)

            def taps(p, n):
                g = 2 * n + p
                dve.wait_ge(lh_done, g + 1)
                V.scalar_tensor_tensor(out=hl[p][:, :, 1:SEQ], in0=xT[p][:, :, 0:SEQ - 1], scalar=cols[:, 3:4],
                                       in1=hl[p][:, :, 1:SEQ], op0=ALU.mult, op1=ALU.add).then_inc(tap_done, 1)
                dve.wait_ge(tap_done, g + 1)
                V.scalar_tensor_tensor(out=hl[p][:, :, 0:SEQ - 1], in0=xT[p][:, :, 1:SEQ], scalar=cols[:, 5:6],
                                       in1=hl[p][:, :, 0:SEQ - 1], op0=ALU.mult, op1=ALU.add).then_inc(hl_done, 1)

            def add(p, n):
                g = 2 * n + p
                dve.wait_ge(hl_done, g + 1)
                dve.wait_ge(ot_done[0], g + 1)
                dve.wait_ge(ot_done[1], g + 1)
                V.tensor_tensor(h2T[:, bass.ds(g * GN, GN)].rearrange("p (b t) -> p b t", b=2), ot[:], hl[p][:],
                                ALU.add).then_inc(h2_done, 1)

            def group(p, n, first=False, last=False):
                g = 2 * n + p
                before = (1 - p, n - 1 if p == 0 else n)
                behind = (1 - p, n if p == 0 else n + 1)
                bias(g, 0)
                bias(g, 1)
                elu(g, 0)
                cosine(g, 0)
                bias(g, 2)
                elu(g, 1)
                cosine(g, 1)
                bias(g, 3)
                rotated(g, 0)
                elu(g, 2)
                cosine(g, 2)
                if not first:
                    center2(*before)
                rotated(g, 1)
                elu(g, 3)
                cosine(g, 3)
                rotated(g, 2)
                if not last:
                    patch(*behind)
                heads(g, 0)
                rotated(g, 3)
                if not last:
                    center1(*behind)
                if not first:
                    norm2(*before)
                taps(p, n)
                heads(g, 1)
                attended(g, 0)
                if not last:
                    norm1(*behind)
                attended(g, 1)
                add(p, n)

            dve.wait_ge(s_small, 160)
            dve.wait_ge(s_cst, 16)
            for i in range(2):
                V.tensor_tensor(hT[i][:, :, 0], cols[:, 1:2].broadcast_to([P, 2]),
                                pos_sb[:, 0:1].broadcast_to([P, 2]), ALU.mult).then_inc(cls_ready, 1)
            V.memset(sc[:], 0.0).then_inc(cls_ready, 1)
            patch(0, 0)
            center1(0, 0)
            norm1(0, 0)
            group(0, 0, first=True)
            with dve.Fori(0, G // 2 - 1) as i:
                n = dve.snap(i)
                group(1, n)
                group(0, n + 1)
            group(1, G // 2 - 1, last=True)
            center2(1, G // 2 - 1)
            norm2(1, G // 2 - 1)

            steps = [0]
            chain = route_chain

            def then(ins):
                steps[0] += 1
                ins.then_inc(chain, 1)
                dve.wait_ge(chain, steps[0])

            def per_tile(ap):
                return ap.rearrange("p (j o) -> p j o", o=1).broadcast_to([P, J, E])

            def per_expert(ap):
                return ap.rearrange("p (o e) -> p o e", o=1).broadcast_to([P, J, E])

            def first_best(scores, best, one_hot):
                then(V.tensor_reduce(best, scores, AX.X, ALU.max))
                then(V.tensor_tensor(eq[:], scores, per_tile(best), ALU.is_equal))
                then(V.tensor_tensor(wk[:], eq[:], per_expert(cst[:, C_RANK:C_RANK + E]), ALU.mult))
                then(V.tensor_reduce(rk[:], wk[:], AX.X, ALU.max))
                then(V.tensor_tensor(one_hot, wk[:], per_tile(rk[:]), ALU.is_equal))

            def without(scores, one_hot):
                then(V.scalar_tensor_tensor(out=scores, in0=one_hot, scalar=-1e30, in1=scores,
                                            op0=ALU.mult, op1=ALU.add))

            dve.wait_ge(gate_done, 1)
            dve.wait_ge(cls_ready, 3)
            then(V.tensor_copy(sc[:, 0:J - 1, :], bank[0][:, 0:(J - 1) * E].rearrange("p (j e) -> p j e", e=E)))
            then(V.tensor_copy(sc[0:LAST, J - 1, :], bank[0][0:LAST, (J - 1) * E:J * E]))
            then(V.tensor_tensor(scb[:], sc[:], per_expert(gateb_sb[:]), ALU.add))
            first_best(scb[:], mx[:], pick[:, 0])
            without(scb[:], pick[:, 0])
            first_best(scb[:], mx[:], pick[:, 1])
            then(V.tensor_tensor(both[:], pick[:, 0], pick[:, 1], ALU.add))
            both_inc = V.tensor_copy(wk[:], both[:])
            both_inc.then_inc(both_ready, 1)
            first_best(sc[:], top[:, 0, :], pick_u[:])
            without(sc[:], pick_u[:])
            V.tensor_reduce(top[:, 1, :], sc[:], AX.X, ALU.max).then_inc(route, 1)
            dve.wait_ge(sg_e, 1)
            then(V.tensor_scalar(sg[:], sg[:], 1.0, None, ALU.add))
            then(V.reciprocal(sg[:], sg[:]))
            then(V.tensor_tensor(mx[:], sg[:, 0, :], sg[:, 1, :], ALU.add))
            then(V.reciprocal(mx[:], mx[:]))
            dve.wait_ge(ids_ready, 1)
            for k in range(2):
                last = V.tensor_tensor(xd[:, :, k, D + 1], sg[:, k, :], mx[:], ALU.mult)
            last.then_inc(weight_done, 1)
            dve.wait_ge(pref_done, 1)
            then(V.tensor_copy(cnt[:], bank[2][:, 0:J * E].rearrange("p (j e) -> p e j", e=E)))
            then(V.tensor_tensor_scan(inc[:].rearrange("p e j -> p (e j)"), cst[:, C_RESET:C_RESET + E * J],
                                      cnt[:].rearrange("p e j -> p (e j)"), 0.0, ALU.mult, ALU.add))
            then(V.tensor_tensor(exc[:], inc[:], cnt[:], ALU.subtract))
            then(V.tensor_tensor(exc[:], exc[:], cst[:, C_BASE:C_BASE + E].rearrange("p (e o) -> p e o", o=1)
                                 .broadcast_to([P, E, J]), ALU.add))
            then(V.tensor_tensor(place[:], bank[1][:, 0:J * E].rearrange("p (j e) -> p j e", e=E),
                                 exc[:].rearrange("p e j -> p j e"), ALU.add))
            then(V.tensor_tensor(prod[:], pick[:], place[:].rearrange("p (o j) e -> p o j e", o=1)
                                 .broadcast_to([P, 2, J, E]), ALU.mult))
            then(V.tensor_reduce(pos_f[:], prod[:], AX.X, ALU.add))
            V.tensor_copy(pos_i[:], pos_f[:]).then_inc(pos_done, 1)
            n_e = inc[:, :, J - 1]
            then(V.tensor_scalar(tn[:], n_e, float(P - 1), None, ALU.add))
            then(V.tensor_copy(ti[:, 0, :], tn[:]))
            then(V.tensor_scalar(ti[:, 1, :], ti[:, 0, :], 7, None, ALU.arith_shift_right))
            then(V.tensor_copy(tf[:], ti[:, 1, :]))
            then(V.tensor_tensor_scan(te[:], cst[:, C_ONE:C_ONE + E], tf[:], 0.0, ALU.mult, ALU.add))
            def tiles_of(ap):
                return ap.rearrange("p (o e) -> p o e", o=1).broadcast_to([P, TILES, E])
            iota = cst[:, C_IOTA:C_IOTA + TILES]
            then(V.tensor_tensor(ge[:], iota.rearrange("p (t o) -> p t o", o=1).broadcast_to([P, TILES, E]),
                                 tiles_of(te[:]), ALU.is_ge))
            then(V.tensor_reduce(t_e[:], ge[:], AX.X, ALU.add))
            then(V.tensor_tensor(gn[:], ge[:], tiles_of(tf[:]), ALU.mult))
            then(V.tensor_reduce(t_s[:], gn[:], AX.X, ALU.add))
            then(V.tensor_tensor(t_s[:], iota, t_s[:], ALU.subtract))
            then(V.tensor_scalar(t_r[:, 0, :], t_e[:], float(CAP), None, ALU.mult))
            then(V.scalar_tensor_tensor(out=t_r[:, 1, :], in0=t_s[:], scalar=float(P), in1=t_r[:, 0, :],
                                        op0=ALU.mult, op1=ALU.add))
            then(V.tensor_scalar(t_r[:, 1, :], t_r[:, 1, :], float(E * CAP), None, ALU.min))
            then(V.tensor_copy(tab_r[:], t_r[:, 1, :]))
            then(V.tensor_scalar(t_e[:], t_e[:], float(E - 1), float(2 * D), ALU.min, ALU.mult))
            then(V.tensor_copy(tab_e[:], t_e[:]))
            then(V.tensor_tensor(tn[:], n_e, cst[:, C_BASE:C_BASE + E], ALU.add))
            V.tensor_copy(tab_p[:], tn[:]).then_inc(tab_done, 1)

            for j in range(J):
                rows = P if j < J - 1 else LAST
                dve.wait_ge(xd_tr, j + 1)
                V.tensor_copy(xd[0:rows, j, :, 0:D],
                              bank[5 + j % 2][0:rows, 0:D].rearrange("p (o d) -> p o d", o=1)
                              .broadcast_to([rows, 2, D])).then_inc(xd_ready, 1)

            with dve.Fori(0, G) as i:
                g = dve.snap(i)
                for m in range(2):
                    dve.wait_ge(sh_act, 2 * g + m + 1)
                    if m == 0:
                        dve.wait_ge(sh_down, g)
                    V.tensor_tensor(sh_h[m][:], sh_s[m][:], bank[2 + m][:, 0:GN], ALU.mult).then_inc(sh_mul, 1)
                dve.wait_ge(sh_down, g + 1)
                V.tensor_tensor(h2T[:, bass.ds(g * GN, GN)], h2T[:, bass.ds(g * GN, GN)], bank[4][:, 0:GN], ALU.add
                                ).then_inc(sh_add, 1)

            def untransposed(n, u):
                q = u % 2
                dve.wait_ge(tx_done[slot(u, 0)], turns(n, u, 0))
                after(dve, up_done[slot(u, 2)], turns(n, u, 2))
                V.tensor_copy(xsT[q][:], bank[q][:, 0:P]).then_inc(xsT_done[slot(u, 0)], 1)

            def gated(n, u):
                at, q = slot(u, 1), (u - 1) % 2
                dve.wait_ge(silu_done[at], turns(n, u, 1))
                after(dve, th_done[slot(u, 3)], turns(n, u, 3))
                V.tensor_tensor(hm[q][:], hs[q][:], bank[2 + q][:, HID:2 * HID], ALU.mult).then_inc(hm_done[at], 1)

            def dve_step(n, u):
                if exists(n, u, 0):
                    untransposed(n, u)
                if exists(n, u, 1):
                    gated(n, u)

            expert_steps(dve, dve_step, 1)

            for c in range(J // YC):
                n_dma = 4 if c == J // YC - 1 else 2
                dve.wait_ge(y_loaded[c % 2], 16 * (2 * (c // 2) + n_dma))
                if c == 0:
                    dve.wait_ge(res_copied, J)
                if c < J // YC - 1:
                    parts = [(P, 0, YC)]
                else:
                    parts = [(P, 0, YC - 1), (LAST, YC - 1, YC)]
                for rows, a, b in parts:
                    last = V.tensor_tensor(yb[c % 2][0:rows, a:b, :], yb[c % 2][0:rows, a:b, :],
                                           res[0:rows, c * YC + a:c * YC + b, :], ALU.add)
                last.then_inc(fin_a, 1)
                dve.wait_ge(fin_a, c + 1)
                for rows, a, b in parts:
                    last = V.tensor_tensor(ya[c % 2][0:rows, a:b, :], ya[c % 2][0:rows, a:b, :],
                                           yb[c % 2][0:rows, a:b, :], ALU.add)
                last.then_inc(fin_done, 1)

        @block.tensor
        def _(pe):
            M, T = nc.tensor.matmul, nc.tensor.transpose

            def tokens(p, n):
                g = 2 * n + p
                pe.wait_ge(x_loaded[p], 32 * n + 32)
                after(pe, hpatch_done, g)
                for k in range(KB):
                    M(ps_tok[:, 0:P], wt[:, k, :], xp[p][:, k, :], start=(k == 0), stop=False)
                M(ps_tok[:, 0:P], wt_rest[:], xr[p][:], start=False, stop=True).then_inc(tok_done, 1)

            def mean_1(p, n):
                g = 2 * n + p
                pe.wait_ge(hpatch_done, g + 1)
                pe.wait_ge(txt_loaded[p], 16 * n + 16)
                after(pe, lv1_done, g)
                M(ps_ln1[:, 0:GN], mean_w, hT[p][:].rearrange("p b t -> p (b t)"), start=True, stop=True
                  ).then_inc(mean1, 1)

            def var_1(p, n):
                g = 2 * n + p
                pe.wait_ge(sq1_done, g + 1)
                M(ps_ln1[:, 0:GN], mean_w, sq1[:], start=True, stop=True).then_inc(var1, 1)

            def mean_2(p, n):
                g = 2 * n + p
                pe.wait_ge(h2_done, g + 1)
                after(pe, lv2_done, g)
                M(ps_ln2[:, 0:GN], mean_w, h2T[:, bass.ds(g * GN, GN)], start=True, stop=True).then_inc(mean2, 1)

            def var_2(p, n):
                g = 2 * n + p
                pe.wait_ge(sq2_done, g + 1)
                M(ps_ln2[:, 0:GN], mean_w, sq2[:], start=True, stop=True).then_inc(var2, 1)

            def project(p, g, k):
                at, rows, _ = PIECES[k]
                x = xT[p][:].rearrange("p b t -> p (b t)")[:, at:at + rows]
                if k == 0:
                    pe.wait_ge(xT_done, g + 1)
                if k < 2:
                    after(pe, qk_done[k + 2], g)
                    after(pe, v_done[k + 2], g)
                else:
                    pe.wait_ge(qk_done[k - 2], g + 1)
                    pe.wait_ge(v_done[k - 2], g + 1)
                M(ps_qkv[k % 2][0:rows, 0:2 * D], x, wqk_sb[:], start=True, stop=True)
                T(ps_qkv[k % 2][0:rows, 2 * D:3 * D], x, ident).then_inc(qkv_done[k], 1)

            def turn(g, j):
                after(pe, qq_done[1 - j], g + j)
                for k in (2 * j, 2 * j + 1):
                    at, rows = PIECES[k][0] - j * SEQ, PIECES[k][1]
                    pe.wait_ge(ft_done[k], g + 1)
                    T(ps_tr[:, at:at + rows], ft[k][0:rows, 0:D], ident[0:rows, 0:rows])
                    pe.wait_ge(rr_done[k], g + 1)
                    last = T(ps_tr[:, SEQ + at:SEQ + at + rows], rr[k][0:rows, 0:D], ident[0:rows, 0:rows])
                last.then_inc(qT_done[j], 1)

            def sums(g, j):
                after(pe, kvm_done[1 - j], g + j)
                for i, k in enumerate((2 * j, 2 * j + 1)):
                    rows = PIECES[k][1]
                    pe.wait_ge(v_done[k], g + 1)
                    M(ps_kv[:, 0:D], rr[k][0:rows, D:2 * D], vt[k][0:rows, :], start=(i == 0), stop=(i == 1))
                for i, k in enumerate((2 * j, 2 * j + 1)):
                    rows = PIECES[k][1]
                    last = M(ps_kv[:, D:D + 2], ft[k][0:rows, D:2 * D], ones[0:rows, 0:2], start=(i == 0), stop=(i == 1))
                last.then_inc(kv_done[j], 1)

            def attend(g, j):
                pe.wait_ge(kvm_done[j], g + 1)
                pe.wait_ge(qq_done[j], g + 1)
                after(pe, ot_done[1 - j], g + j)
                M(ps_od[:, 0:SEQ], kvm[j][:, 0, :], qq[j][:, 1, :], start=True, stop=True)
                M(ps_od[:, SEQ:2 * SEQ], kvm[j][:, 1, :], qq[j][:, 0, :], start=True, stop=True
                  ).then_inc(od_done[j], 1)

            def group(p, n, first=False, last=False):
                g = 2 * n + p
                before = (1 - p, n - 1 if p == 0 else n)
                behind = (1 - p, n if p == 0 else n + 1)
                for k in range(4):
                    project(p, g, k)
                if not first:
                    mean_2(*before)
                if not last:
                    tokens(*behind)
                turn(g, 0)
                sums(g, 0)
                if not first:
                    var_2(*before)
                if not last:
                    mean_1(*behind)
                turn(g, 1)
                sums(g, 1)
                attend(g, 0)
                if not last:
                    var_1(*behind)
                attend(g, 1)

            pe.wait_ge(s_wtok, 32)
            tokens(0, 0)
            pe.wait_ge(s_cst, 16)
            pe.wait_ge(s_small, 160)
            pe.wait_ge(cls_ready, 2)
            mean_1(0, 0)
            var_1(0, 0)
            group(0, 0, first=True)
            with pe.Fori(0, G // 2 - 1) as i:
                n = pe.snap(i)
                group(1, n)
                group(0, n + 1)
            group(1, G // 2 - 1, last=True)
            mean_2(1, G // 2 - 1)
            var_2(1, G // 2 - 1)

            pe.wait_ge(x2_done, G)
            for j in range(J):
                rows = P if j < J - 1 else LAST
                last = M(bank[0][0:rows, E * j:E * j + E], x2T[:, P * j:P * j + rows], gate_sb[:], start=True, stop=True)
            last.then_inc(gate_done, 1)

            def turn_row(j):
                rows = P if j < J - 1 else LAST
                after(pe, xd_ready, j - 1)
                T(bank[5 + j % 2][0:rows, 0:D], x2T[:, P * j:P * j + rows], ident).then_inc(xd_tr, 1)

            turn_row(0)
            turn_row(1)
            pe.wait_ge(both_ready, 1)
            full = (J - 1) * E
            flat = both[:].rearrange("p j e -> p (j e)")
            M(bank[1][:, 0:full], tri, flat[:, 0:full], start=True, stop=True)
            M(bank[1][:, full:J * E], tri[0:LAST, :], flat[0:LAST, full:J * E], start=True, stop=True)
            M(bank[2][:, 0:full], ones, flat[:, 0:full], start=True, stop=True)
            M(bank[2][:, full:J * E], ones[0:LAST, :], flat[0:LAST, full:J * E], start=True, stop=True
              ).then_inc(pref_done, 1)
            for j in range(2, J):
                turn_row(j)

            pe.wait_ge(s_wexp, 96)
            pe.wait_ge(pos_done, 1)
            with pe.Fori(0, G) as i:
                g = pe.snap(i)
                x = x2T[:, bass.ds(g * GN, GN)]
                pe.wait_ge(sh_mul, 2 * g)
                for m in range(2):
                    M(bank[2 + m][:, 0:GN], sw13[:, HID + P * m:HID + P * m + P], x, start=True, stop=True)
                    M(bank[m][:, 0:GN], sw13[:, P * m:P * m + P], x, start=True, stop=True).then_inc(sh_up, 1)
                pe.wait_ge(sh_add, g)
                for m in range(2):
                    pe.wait_ge(sh_mul, 2 * g + m + 1)
                    last = M(bank[4][:, 0:GN], sw2_sb[:, m, :], sh_h[m][:], start=(m == 0), stop=(m == 1))
                last.then_inc(sh_down, 1)
            pe.wait_ge(sh_add, G)
            for j in range(J):
                rows = P if j < J - 1 else LAST
                after(pe, res_copied, j - 1)
                T(bank[6 + j % 2][0:rows, 0:D], h2T[:, P * j:P * j + rows], ident).then_inc(res_tr, 1)

            pe.wait_ge(tab_done, 1)

            at_w2 = [pe.alloc_register(f"at_w2_{u}") for u in range(U)]
            tile_no = pe.alloc_register("tile_no")
            pe.reg_mov(tile_no, 0)

            def transposed(n, u):
                q = u % 2
                t = pe.snap(tile_no, min_val=0, max_val=TILES - 1) if not isinstance(n, int) else U * n + u
                pe.reg_load(at_w2[u], tab_e[0:1, bass.ds(t, 1)])
                pe.reg_add(tile_no, tile_no, 1)
                pe.wait_ge(xs_loaded[u], 16 * n + 16 if isinstance(n, int) else loaded)
                after(pe, xsT_done[slot(u, 2)], turns(n, u, 2))
                T(bank[q][:, 0:P], xs[u][:, 0:D], ident).then_inc(tx_done[slot(u, 0)], 1)

            def up(n, u):
                at, q = slot(u, 1), (u - 1) % 2
                w = w13[:].rearrange("p e h -> p (e h)")
                first = pe.snap(at_w2[(u - 1) % U], min_val=0, max_val=(E - 1) * 2 * D)
                pe.wait_ge(xsT_done[at], turns(n, u, 1))
                after(pe, hm_done[slot(u, 3)], turns(n, u, 3))
                M(bank[2 + q][:, 0:2 * HID], xsT[q][:], w[:, bass.ds(first * 2, 2 * HID)],
                  start=True, stop=True).then_inc(up_done[at], 1)

            def hidden(n, u):
                at, q = slot(u, 2), u % 2
                pe.wait_ge(hm_done[at], turns(n, u, 2))
                after(pe, hmT_done[slot(u, 4)], turns(n, u, 4))
                for m in range(2):
                    last = T(bank[4 + q][:, P * m:P * m + P], hm[q][:, P * m:P * m + P], ident)
                last.then_inc(th_done[at], 1)

            def down(n, u):
                at, q = slot(u, 3), (u - 1) % 2
                w = w2_sb[:].rearrange("p e k d -> p (e k d)")
                first = pe.snap(at_w2[(u - 3) % U], min_val=0, max_val=(E - 1) * 2 * D)
                pe.wait_ge(hmT_done[at], turns(n, u, 3))
                after(pe, ys_done[slot(u, 5)], turns(n, u, 5))
                for m in range(2):
                    last = M(bank[6 + q][:, 0:D], hmT[q][:, m, :], w[:, bass.ds(first + m * D, D)],
                             start=(m == 0), stop=(m == 1))
                last.then_inc(dn_done[at], 1)

            loaded = pe.alloc_register("loaded")
            pe.reg_mov(loaded, 16)

            def pe_step(n, u):
                if exists(n, u, 1):
                    up(n, u)
                if u == 0 and not isinstance(n, int):
                    pe.reg_add(loaded, loaded, 16)
                if exists(n, u, 0):
                    transposed(n, u)
                if exists(n, u, 2):
                    hidden(n, u)
                if exists(n, u, 3):
                    down(n, u)

            pe.wait_ge(res_copied, J)
            expert_steps(pe, pe_step, 3)


_OUT = (NTOK, D)


def kernel(x, txt, L0_tok_W, L0_tok_b, L0_tok_class_token, L0_tok_pos_embed, L0_attn_Wqk, L0_attn_bqk,
           L0_attn_lepe_w, L0_attn_lepe_b, L0_ffn_gate_w, L0_ffn_biases, L0_ffn_w1, L0_ffn_w3, L0_ffn_w2,
           L0_ffn_sw1, L0_ffn_sw3, L0_ffn_sw2):
    import concourse.bacc as bacc
    from concourse.bass_utils import run_bass_kernel_spmd

    con = np.ascontiguousarray
    patches = x.reshape(G, 2, CH, GRID, PATCH, GRID, PATCH).transpose(0, 2, 4, 6, 1, 3, 5)
    arrays = {
        "patches": con(patches).reshape(G * IN_D, 2 * NP_),
        "txt": con(txt.transpose(2, 0, 1)).reshape(D, B * NT),
        "w_tok": con(L0_tok_W.transpose(1, 0)),
        "b_tok": L0_tok_b.reshape(D, 1),
        "cls": L0_tok_class_token.reshape(D, 1),
        "pos": con(L0_tok_pos_embed.transpose(1, 0)),
        "wqk": con(L0_attn_Wqk),
        "bqk": L0_attn_bqk.reshape(1, 2 * D),
        "lepe_w": L0_attn_lepe_w.reshape(D, 3),
        "lepe_b": L0_attn_lepe_b.reshape(D, 1),
        "gate_w": con(L0_ffn_gate_w.transpose(1, 0)),
        "gate_b": L0_ffn_biases.reshape(1, E),
        "w1": con(L0_ffn_w1), "w3": con(L0_ffn_w3), "w2": con(L0_ffn_w2),
        "sw1": con(L0_ffn_sw1), "sw3": con(L0_ffn_sw3), "sw2": con(L0_ffn_sw2),
        "consts": constants(),
        "dests": destinations(),
    }
    arrays = {f"in_{k}": np.asarray(v) for k, v in arrays.items()}
    nc = bacc.Bacc("TRN2", target_bir_lowering=False, num_devices=1)
    args = [nc.dram_tensor(k, a.shape, mybir.dt.from_np(a.dtype), kind="ExternalInput").ap()
            for k, a in arrays.items()]
    args.append(nc.dram_tensor("out_tokens", _OUT, F32, kind="ExternalOutput").ap())
    build(nc, *args)
    r = run_bass_kernel_spmd(nc, [arrays], core_ids=[0])
    return np.asarray(r.results[0]["out_tokens"]).reshape(B, SEQ, D)
```

```python
import numpy as np
import concourse.bass as bass
from concourse import mybir
from contextlib import ExitStack

F32 = mybir.dt.float32
F32R = mybir.dt.float32r
I32 = mybir.dt.int32
U32 = mybir.dt.uint32
ALU = mybir.AluOpType
ACT = mybir.ActivationFunctionType
AX = mybir.AxisListType

P = 128
B, CH, IMG, GRID = 16, 3, 224, 8
PATCH = IMG // GRID
IN_D = CH * PATCH * PATCH
KB = IN_D // P
KR = IN_D - KB * P
D = 128
NP_, NT = GRID * GRID, 128
SEQ = 1 + NP_ + NT
NTOK = B * SEQ
H, HD = 8, 16
G = B // 2
GN = 2 * SEQ
LN_EPS, Z_EPS = 1e-5, 1e-6
E, HID = 8, 256
PIECES = [(0, 1 + NP_, 0), (1 + NP_, NT, 1), (SEQ, 1 + NP_, 0), (SEQ + 1 + NP_, NT, 1)]
J = -(-NTOK // P)
LAST = NTOK - (J - 1) * P
JA = (G // 2) * GN // P
BATCH = 4
CAP = NTOK + P
TILES = (2 * NTOK - E) // P + E
DEAD = TILES - (2 * NTOK) // P
ROW = D + 1
BIG = 1 << 20
U = 8
SLOTS = 2
FIRST = [(0, 4), (4, 9), (9, 14), (14, KB)]
FIRST_AT = {a: i for i, (a, _) in enumerate(FIRST)}
assert JA % BATCH == 0 and E == G
assert TILES % U == 0 and U % SLOTS == 0 and G % 2 == 0

C_ID, C_MEAN, C_TRI, C_ONE, C_MASK = 0, P, 2 * P, 3 * P, 4 * P
C_COS = 5 * P
C_SIN = C_COS + 2 * HD
C_RANK = C_SIN + 2 * HD
C_RESET = C_RANK + E
C_BASE = C_RESET + E * J
C_IOTA = C_BASE + E
C_CENTER = C_IOTA + TILES
NCONST = C_CENTER + P


def constants():
    c = np.zeros((P, NCONST), np.float32)
    c[:, C_ID:C_ID + P] = np.eye(P)
    c[:, C_MEAN:C_MEAN + P] = 1.0 / D
    c[:, C_CENTER:C_CENTER + P] = np.eye(P) - 1.0 / D
    c[:, C_TRI:C_TRI + P] = np.triu(np.ones((P, P)), 1)
    c[:, C_ONE:C_ONE + P] = 1.0
    head = np.arange(P) // HD
    c[:, C_MASK:C_MASK + P] = (head[:, None] == head[None, :]) / SEQ
    inv = 1.0 / 10000.0 ** (np.arange(0, HD, 2, dtype=np.float32) / HD)
    freq = np.outer(np.arange(SEQ, dtype=np.float32), inv).astype(np.float32)
    cos, sin = np.cos(freq), np.sin(freq)
    for half, (start, rows) in enumerate(((0, 1 + NP_), (1 + NP_, NT))):
        at = slice(start, start + rows)
        c[:rows, C_COS + HD * half:C_COS + HD * half + HD] = np.concatenate([cos[at], cos[at]], 1)
        c[:rows, C_SIN + HD * half:C_SIN + HD * half + HD] = np.concatenate([-sin[at], sin[at]], 1)
    c[:, C_RANK:C_RANK + E] = np.arange(E, 0, -1)
    for first, end in ((0, JA), (JA, J)):
        reset = np.ones((E, end - first))
        reset[:, 0] = 0
        c[:, C_RESET + E * first:C_RESET + E * end] = reset.reshape(-1)
    c[:, C_BASE:C_BASE + E] = np.arange(E) * CAP
    c[:, C_IOTA:C_IOTA + TILES] = np.arange(TILES)
    return c


def destinations():
    flat = np.arange(J)[None, :, None] * P + np.arange(P)[:, None, None]
    ids = flat + np.arange(2)[None, None, :] * NTOK
    return np.concatenate([ids.reshape(P, 2 * J), np.full((P, 1), BIG)], 1).astype(np.int32)


def build(nc, patches, txt, w_tok, b_tok, cls, pos, wqk, bqk, lepe_w, lepe_b, gate_w, gate_b,
          w1, w3, w2, sw1, sw3, sw2, consts, dests, out):
    xs_dram = nc.dram_tensor("xs_dram", [E * CAP + DEAD * P, ROW], F32).ap()
    y_dram = nc.dram_tensor("y_dram", [2 * NTOK, D], F32).ap()
    ctx = ExitStack()
    with ctx:
        def sb(name, shape, dt=F32):
            return ctx.enter_context(nc.sbuf_tensor(name, shape, dt))

        def pb(name):
            return ctx.enter_context(nc.psum_tensor(name, [P, 512], F32))

        def sem(name):
            return ctx.enter_context(nc.semaphore(name))

        def sems(name, n):
            return [sem(f"{name}{i}") for i in range(n)]

        cst = sb("cst", [P, NCONST])
        ident, mean_w = cst[:, C_ID:C_ID + P], cst[:, C_MEAN:C_MEAN + P]
        center_w = cst[:, C_CENTER:C_CENTER + P]
        tri, ones, mask = cst[:, C_TRI:C_TRI + P], cst[:, C_ONE:C_ONE + P], cst[:, C_MASK:C_MASK + P]
        dest_sb = sb("dest_sb", [P, 2 * J + 1], I32)
        wt = sb("wt", [P, KB, D])
        wt_rest = sb("wt_rest", [KR, D])
        cols = sb("cols", [P, 8])
        pos_sb = sb("pos_sb", [P, 1 + NP_])
        wqk_sb = sb("wqk_sb", [P, 2 * D])
        bqk_sb = sb("bqk_sb", [P, 2 * D])
        gate_sb = sb("gate_sb", [P, E])
        gateb_sb = sb("gateb_sb", [P, E])
        w13 = sb("w13", [P, E, 2 * HID])
        w2_sb = sb("w2_sb", [P, E, 2, D])
        sw13 = sb("sw13", [P, 2 * HID])
        sw2_sb = sb("sw2_sb", [P, 2, D])

        xp_both = sb("xp_both", [P, 2, KB, P])
        xp = [xp_both[:, i] for i in range(2)]
        xr = [sb(f"xr{i}", [KR, P]) for i in range(2)]
        hT = [sb(f"hT{i}", [P, 2, SEQ]) for i in range(2)]
        sq1, lv1, rs1 = (sb(n, [P, GN]) for n in ("sq1", "lv1", "rs1"))
        sq2, lv2, rs2 = (sb(n, [P, GN]) for n in ("sq2", "lv2", "rs2"))
        xT = [sb(f"xT{i}", [P, 2, SEQ]) for i in range(2)]
        att = sb("att", [P, 5, 4, 2 * D])
        qk, ex, ss, ft, rr = ([att[:, i, k, :] for k in range(4)] for i in range(5))
        cc = ex
        vt = [sb(f"vt{k}", [P, D]) for k in range(4)]
        qq = [sb(f"qq{j}", [P, 2, SEQ]) for j in range(2)]
        kvm = [sb(f"kvm{j}", [P, 2, D]) for j in range(2)]
        zt = [sb(f"zt{j}", [P, SEQ]) for j in range(2)]
        zr = [sb(f"zr{j}", [P, SEQ]) for j in range(2)]
        ot = sb("ot", [P, 2, SEQ])
        hl = [sb(f"hl{i}", [P, 2, SEQ]) for i in range(2)]
        h2T = sb("h2T", [P, NTOK])
        x2T = sb("x2T", [P, NTOK])

        bank = [pb(f"bank{i}") for i in range(8)]
        ps_var, ps_dev2, ps_tok, ps_dev1 = bank[0], bank[1], bank[2], bank[2]
        ps_qkv, ps_tr, ps_kv, ps_od = bank[3:5], bank[5], bank[6], bank[7]

        ps_gate, ps_before, ps_total = bank[2], bank[1], bank[0]
        ps_ahead, ps_rows = bank[3], bank[4]

        sc = sb("sc", [P, J, E])
        scb = sb("scb", [P, J, E])
        eq = sb("eq", [P, J, E])
        wk = sb("wk", [P, J, E])
        pick = sb("pick", [P, 2, J, E])
        pick_u = sb("pick_u", [P, J, E])
        top = sb("top", [P, 2, J])
        mx = sb("mx", [P, J])
        rk = sb("rk", [P, J])
        sg = sb("sg", [P, 2, J])
        weight = sb("weight", [P, 2, J])
        both = sb("both", [P, J, E])
        cnt, inc, exc = ([sb(f"{name}{i}", [P, E, n]) for i, n in enumerate((JA, J - JA))]
                         for name in ("cnt", "inc", "exc"))
        cnt_on = sb("cnt_on", [P, E, J - JA])
        place = sb("place", [P, J, E])
        prod = sb("prod", [P, 2, J, E])
        pos_f = sb("pos_f", [P, 2, J])
        pos_i = sb("pos_i", [P, 2, J], I32)
        tn = sb("tn", [P, E])
        ti = sb("ti", [P, 2, E], I32)
        tf = sb("tf", [P, E])
        te = sb("te", [P, E])
        ge = sb("ge", [P, TILES, E])
        gn = sb("gn", [P, TILES, E])
        t_e = sb("t_e", [P, TILES])
        t_s = sb("t_s", [P, TILES])
        t_r = sb("t_r", [P, 2, TILES])
        tab_e = sb("tab_e", [P, TILES], I32)
        tab_r = sb("tab_r", [P, TILES], I32)
        tab_p = sb("tab_p", [P, E], I32)
        xd = sb("xd", [P, J, 2, ROW])
        pad = sb("pad", [P, ROW])

        xs = [sb(f"xs{u}", [P, ROW]) for u in range(U)]
        xsT_h = [sb(f"xsT_h{u}", [P, P], F32R) for u in range(2)]
        xsT_l = [sb(f"xsT_l{u}", [P, P], F32R) for u in range(2)]
        w13_flat = w13[:].rearrange("p e h -> p (e h)")
        w13_l = w13_flat.bitcast(F32R)
        w13_h = xp_both[:].rearrange("p i k t -> p (i k t)")[:, 0:E * 2 * HID].bitcast(F32R)
        hs = [sb(f"hs{u}", [P, HID]) for u in range(2)]
        hm = [sb(f"hm{u}", [P, HID]) for u in range(2)]
        hmT = [sb(f"hmT{u}", [P, 2, P]) for u in range(2)]
        ys = [sb(f"ys{u}", [P, D]) for u in range(U)]
        goal = [sb(f"goal{u}", [P, ROW - D]) for u in range(U)]
        sh_s = [lv1, sq1]
        sh_h = [lv2, sq2]
        YC = 5
        result_rows = xd[:].rearrange("p j k r -> p (j k r)")[:, 0:2 * J * D].rearrange("p (k j d) -> p k j d", k=2, d=D)
        res = att[:].rearrange("p a k c -> p (a k c)")[:, 0:J * D].rearrange("p (j d) -> p j d", d=D)

        first_loaded = sems("first_loaded", len(FIRST))
        s_cst, s_wtok, s_small, s_wexp = sem("s_cst"), sem("s_wtok"), sem("s_small"), sem("s_wexp")
        x_loaded, txt_loaded = sems("x_loaded", 2), sems("txt_loaded", 2)
        cls_ready = sem("cls_ready")
        tok_done, hpatch_done = sem("tok_done"), sem("hpatch_done")
        dev1_done, sq1_done, var1, lv1_done, rs1_done = (
            sem(n) for n in ("dev1_done", "sq1_done", "var1", "lv1_done", "rs1_done"))
        dev2_done, sq2_done, var2, lv2_done, rs2_done = (
            sem(n) for n in ("dev2_done", "sq2_done", "var2", "lv2_done", "rs2_done"))
        xT_done, x2_done = sem("xT_done"), sem("x2_done")
        qkv_done, qk_done, v_done = sems("qkv_done", 4), sems("qk_done", 4), sems("v_done", 4)
        ex_done, ft_done = sems("ex_done", 4), sems("ft_done", 4)
        cc_done, ss_done, rr_done = sems("cc_done", 4), sems("ss_done", 4), sems("rr_done", 4)
        qT_done, qq_done = sems("qT_done", 2), sems("qq_done", 2)
        kv_done, kvm_done, od_done = sems("kv_done", 2), sems("kvm_done", 2), sems("od_done", 2)
        zt_done, zr_done, ot_done = sems("zt_done", 2), sems("zr_done", 2), sems("ot_done", 2)
        lc_done, lh_done, tap_done, hl_done, h2_done = (
            sem(n) for n in ("lc_done", "lh_done", "tap_done", "hl_done", "h2_done"))
        ids_ready, pad_ready = sem("ids_ready"), sem("pad_ready")
        gate_done, route, sg_e, both_ready, pref_done, pos_done = (
            sem(n) for n in ("gate_done", "route", "sg_e", "both_ready", "pref_done", "pos_done"))
        ahead_read = sem("ahead_read")
        weight_done, scaled, tab_done, route_chain = sem("weight_done"), sem("scaled"), sem("tab_done"), sem("route_chain")
        xd_tr, xd_copied = sem("xd_tr"), sem("xd_copied")
        xd_ready = sem("xd_ready")
        scattered, padded = sem("scattered"), sem("padded")
        sh_up, sh_act, sh_mul, sh_down, sh_add = (
            sem(n) for n in ("sh_up", "sh_act", "sh_mul", "sh_down", "sh_add"))
        res_tr, res_copied = sem("res_tr"), sem("res_copied")
        wh_done, wl_done, xh_done = sem("wh_done"), sem("wl_done"), sem("xh_done")
        xs_loaded = sems("xs_loaded", U)
        tx_done, xsT_done, up_done, silu_done, hm_done, th_done, hmT_done, dn_done, ys_done = (
            sems(n, SLOTS) for n in ("tx_done", "xsT_done", "up_done", "silu_done", "hm_done", "th_done",
                                 "hmT_done", "dn_done", "ys_done"))
        y_sent = sems("y_sent", U)
        y_loaded = [sems(f"y_loaded{k}_", J // YC) for k in range(2)]
        fin_v, fin_p, fin_done, out_sent = sem("fin_v"), sem("fin_p"), sem("fin_done"), sem("out_sent")

        ON_DVE = 3

        def chunk_parts(c):
            if c < J // YC - 1:
                return [(P, c * YC, c * YC + YC)]
            return [(P, c * YC, J - 1), (LAST, J - 1, J)]

        block = ctx.enter_context(nc.Block())

        def after(eng, s, value):
            if not isinstance(value, int) or value > 0:
                eng.wait_ge(s, value)

        def slot(u, back):
            return (u - back) % SLOTS

        def turns(n, u, back):
            k = (u - back) // SLOTS + 1
            return n * (U // SLOTS) + k if isinstance(n, int) else n[k]

        def exists(n, u, back):
            return not isinstance(n, int) or 0 <= U * n + u - back < TILES

        def expert_steps(eng, step, depth):
            for u in range(U):
                step(0, u)
            regs = {k: eng.alloc_register(f"turn{k + 2}") for k in range(-2, U // SLOTS + 1)}
            for k in regs:
                eng.reg_mov(regs[k], U // SLOTS + k)
            with eng.Fori(1, TILES // U):
                for u in range(U):
                    step(regs, u)
                for k in regs:
                    eng.reg_add(regs[k], regs[k], U // SLOTS)
            for u in range(depth):
                step(TILES // U, u)

        def two(eng, body):
            body(0, 0)
            with eng.Fori(0, G // 2 - 1) as i:
                n = eng.snap(i)
                body(1, n)
                body(0, n + 1)
            body(1, G // 2 - 1)

        @block.sync
        def _(sp):
            def load_group(p, n):
                g = 2 * n + p
                at, rest, tokens, old = [
                    v if isinstance(v, int) else sp.snap(v)
                    for v in (g * IN_D, g * IN_D + KB * P, g * 2 * NT, g - 1)]
                after(sp, tok_done, old)
                sp.dma_start(xp[p], patches[bass.ds(at, KB * P), :].rearrange(
                    "(q k) t -> q k t", k=KB)).then_inc(x_loaded[p], 16)
                sp.dma_start(xr[p][:], patches[bass.ds(rest, KR), :]).then_inc(x_loaded[p], 16)
                after(sp, lh_done, old)
                sp.dma_start(hT[p][:, :, 1 + NP_:SEQ], txt[:, bass.ds(tokens, 2 * NT)].rearrange(
                    "c (b t) -> c b t", b=2)).then_inc(txt_loaded[p], 16)

            w_of_block = w_tok[0:KB * P, :].rearrange("(q k) h -> q k h", k=KB)
            x_of_block = patches[0:KB * P, :].rearrange("(q k) t -> q k t", k=KB)
            for i, (a, b) in enumerate(FIRST):
                sp.dma_start(wt[:, a:b, :], w_of_block[:, a:b, :]).then_inc(first_loaded[i], 16)
                sp.dma_start(xp[0][:, a:b, :], x_of_block[:, a:b, :]).then_inc(first_loaded[i], 16)
            sp.dma_start(wt_rest[:], w_tok[KB * P:IN_D, :]).then_inc(s_wtok, 16)
            sp.dma_start(xr[0][:], patches[KB * P:IN_D, :]).then_inc(s_wtok, 16)
            sp.dma_start(hT[0][:, :, 1 + NP_:SEQ], txt[:, 0:2 * NT].rearrange("c (b t) -> c b t", b=2)
                         ).then_inc(txt_loaded[0], 16)
            load_group(1, 0)
            with sp.Fori(1, G // 2) as i:
                for p in range(2):
                    load_group(p, sp.snap(i))

            sp.wait_ge(pad_ready, 2)
            sp.dma_start(xs_dram[E * CAP:, :].rearrange("(k q) r -> q k r", q=P),
                         pad[:].rearrange("p (o r) -> p o r", o=1).broadcast_to([P, DEAD, ROW])
                         ).then_inc(padded, 16)
            sp.wait_ge(tab_done, 1)
            for e in range(E):
                row = sp.value_load(tab_p[0:1, e:e + 1], min_val=0, max_val=E * CAP - P)
                sp.dma_start(xs_dram[bass.ds(row, P), :], pad[:]).then_inc(padded, 16)

            sp.wait_ge(scattered, 16 * 2 * J)
            sp.wait_ge(padded, 16 * (E + 1))

            used = [sp.alloc_register(f"used{k}") for k in range(U // SLOTS)]

            def load_tiles(n, first=False):
                for u in range(U):
                    row = sp.value_load(tab_r[0:1, bass.ds(U * n + u, 1)], min_val=0, max_val=E * CAP)
                    if not first:
                        sp.wait_ge(hm_done[u % SLOTS], used[u // SLOTS])
                    sp.dma_start(xs[u][:], xs_dram[bass.ds(row, P), :]).then_inc(xs_loaded[u], 16)

            load_tiles(0, first=True)
            for k in range(U // SLOTS):
                sp.reg_mov(used[k], k + 1)
            with sp.Fori(1, TILES // U) as n:
                load_tiles(sp.snap(n))
                for k in range(U // SLOTS):
                    sp.reg_add(used[k], used[k], U // SLOTS)

            for u in range(U):
                sp.wait_ge(y_sent[u], 16 * (TILES // U))
            for k in (1, 0):
                for c in range(J // YC):
                    rows = YC * P if c < J // YC - 1 else (YC - 1) * P
                    at = k * NTOK + c * YC * P
                    sp.dma_start(result_rows[:, k, c * YC:c * YC + rows // P, :], y_dram[at:at + rows, :].rearrange(
                        "(j q) d -> q j d", q=P)).then_inc(y_loaded[k][c], 16)
                    if rows < YC * P:
                        sp.dma_start(result_rows[0:LAST, k, J - 1, :], y_dram[at + rows:at + rows + LAST, :]
                                     ).then_inc(y_loaded[k][c], 16)

            for c in range(J // YC):
                sp.wait_ge(fin_done, c + 1)
                rows = YC * P if c < J // YC - 1 else (YC - 1) * P
                at = c * YC * P
                sp.dma_start(out[at:at + rows, :].rearrange("(j q) d -> q j d", q=P),
                             result_rows[:, 0, c * YC:c * YC + rows // P, :]).then_inc(out_sent, 16)
                if rows < YC * P:
                    sp.dma_start(out[at + rows:NTOK, :], result_rows[0:LAST, 0, J - 1, :]).then_inc(out_sent, 16)
            sp.wait_ge(out_sent, 16 * (J // YC + 1))

        @block.scalar
        def _(act):
            A = nc.scalar.activation
            act.dma_start(cst[:], consts[:, :]).then_inc(s_cst, 16)
            act.dma_start(cols[:, 0:1], b_tok[:, :]).then_inc(s_small, 16)
            act.dma_start(cols[:, 1:2], cls[:, :]).then_inc(s_small, 16)
            act.dma_start(cols[:, 2:3], lepe_b[:, :]).then_inc(s_small, 16)
            act.dma_start(cols[:, 3:6], lepe_w[:, :]).then_inc(s_small, 16)
            act.dma_start(pos_sb[:], pos[:, :]).then_inc(s_small, 16)
            act.dma_start(wqk_sb[:], wqk[:, :]).then_inc(s_small, 16)
            act.dma_start(bqk_sb[:], bqk[:, :].broadcast_to([P, 2 * D])).then_inc(s_small, 16)
            act.dma_start(gate_sb[:], gate_w[:, :]).then_inc(s_small, 16)
            act.dma_start(gateb_sb[:], gate_b[:, :].broadcast_to([P, E])).then_inc(s_small, 16)
            act.dma_start(dest_sb[:], dests[:, :]).then_inc(s_small, 16)

            def square1(g):
                act.wait_ge(dev1_done, g + 1)
                A(sq1[:], ps_dev1[:, 0:GN], ACT.Square).then_inc(sq1_done, 1)

            def rstd1(g):
                act.wait_ge(var1, g + 1)
                A(lv1[:], ps_var[:, 0:GN], ACT.Ln, bias=LN_EPS).then_inc(lv1_done, 1)
                act.wait_ge(lv1_done, g + 1)
                A(rs1[:], lv1[:], ACT.Exp, scale=-0.5).then_inc(rs1_done, 1)

            def square2(g):
                act.wait_ge(dev2_done, g + 1)
                A(sq2[:], ps_dev2[:, 0:GN], ACT.Square).then_inc(sq2_done, 1)

            def rstd2(g):
                act.wait_ge(var2, g + 1)
                A(lv2[:], ps_var[:, 0:GN], ACT.Ln, bias=LN_EPS).then_inc(lv2_done, 1)
                act.wait_ge(lv2_done, g + 1)
                A(rs2[:], lv2[:], ACT.Exp, scale=-0.5).then_inc(rs2_done, 1)

            def piece(g, k):
                n = PIECES[k][1]
                act.wait_ge(qk_done[k], g + 1)
                after(act, kv_done[k // 2], g)
                nc.scalar.copy(vt[k][0:n, :], ps_qkv[k % 2][0:n, 2 * D:3 * D]).then_inc(v_done[k], 1)
                A(ex[k][0:n, :], qk[k][0:n, :], ACT.Exp, bias=-1.0).then_inc(ex_done[k], 1)

            def queries(g, j):
                act.wait_ge(qT_done[j], g + 1)
                nc.scalar.copy(qq[j][:], ps_tr[:, 0:GN]).then_inc(qq_done[j], 1)

            def inverse(g, j):
                act.wait_ge(od_done[j], g + 1)
                if j == 0:
                    after(act, ot_done[0], g)
                A(zt[j][:], ps_od[:, SEQ:2 * SEQ], ACT.Ln, bias=Z_EPS).then_inc(zt_done[j], 1)
                act.wait_ge(zt_done[j], g + 1)
                A(zr[j][:], zt[j][:], ACT.Exp, scale=-1.0).then_inc(zr_done[j], 1)

            def rows_ahead(i):
                act.wait_ge(xd_tr, i + 1)
                at = slice(BATCH * i, BATCH * (i + 1))
                nc.scalar.copy(xd[:, at, :, 0:D], ps_rows[:].rearrange("p (j o d) -> p j o d", o=1, d=D)
                               .broadcast_to([P, BATCH, 2, D])).then_inc(xd_ready, 1)

            def group(p, n, first=False, last=False):
                g = 2 * n + p
                piece(g, 0)
                piece(g, 1)
                if not first:
                    queries(g - 1, 1)
                A(hl[p][:], xT[p][:], ACT.Identity, bias=cols[:, 2:3], scale=cols[:, 4:5]).then_inc(lc_done, 1)
                if not first:
                    inverse(g - 1, 1)
                piece(g, 2)
                piece(g, 3)
                if not first:
                    square2(g - 1)
                if not last:
                    square1(g + 1)
                queries(g, 0)
                if not last:
                    rstd1(g + 1)
                inverse(g, 0)
                if not first:
                    rstd2(g - 1)

            act.preload_act_table_set("natural_log_exp_and_others")
            act.wait_ge(s_small, 160)
            square1(0)
            rstd1(0)
            act.dma_start(sw13[:, 0:HID], sw1[:, :]).then_inc(s_wexp, 16)
            act.dma_start(sw13[:, HID:2 * HID], sw3[:, :]).then_inc(s_wexp, 16)
            act.dma_start(sw2_sb[:], sw2.rearrange("(k q) d -> q k d", q=P)).then_inc(s_wexp, 16)
            act.dma_start(w13[:, :, 0:HID], w1.rearrange("e d h -> d e h")).then_inc(s_wexp, 16)
            act.dma_start(w13[:, :, HID:2 * HID], w3.rearrange("e d h -> d e h")).then_inc(s_wexp, 16)
            act.dma_start(w2_sb[:], w2.rearrange("e (k q) d -> q e k d", q=P)).then_inc(s_wexp, 16)
            group(0, 0, first=True)
            with act.Fori(0, G // 2 - 1) as i:
                n = act.snap(i)
                group(1, n)
                group(0, n + 1)
            group(1, G // 2 - 1, last=True)
            queries(G - 1, 1)
            inverse(G - 1, 1)
            square2(G - 1)
            rows_ahead(0)
            rstd2(G - 1)
            for i in range(1, JA // BATCH):
                rows_ahead(i)

            def expert_rows(first, end):
                for j in range(first, end):
                    rows = P if j < J - 1 else LAST
                    act.wait_ge(xd_tr, JA // BATCH + j - JA + 1)
                    nc.scalar.copy(xd[0:rows, j, :, 0:D],
                                   bank[5 + j % 2][0:rows, 0:D].rearrange("p (o d) -> p o d", o=1)
                                   .broadcast_to([rows, 2, D])).then_inc(xd_ready, 1)

            expert_rows(JA, (JA + J) // 2)
            expert_rows((JA + J) // 2, J)

            act.wait_ge(route, 1)
            A(sg[:], top[:], ACT.Exp, scale=-1.0).then_inc(sg_e, 1)

            act.preload_act_table(ACT.Silu)

            def shared_silu(g):
                for m in range(2):
                    act.wait_ge(sh_up, 2 * g + m + 1)
                    after(act, sh_mul, 2 * g - 1 + m)
                    A(sh_s[m][:], bank[m][:, 0:GN], ACT.Silu).then_inc(sh_act, 1)

            def round_w13(e):
                part = bass.ds(e * 2 * HID, 2 * HID)
                nc.scalar.copy(w13_h[:, part], w13_flat[:, part]).then_inc(wh_done, 1)

            act.wait_ge(s_wexp, 96)
            act.wait_ge(tok_done, G)
            shared_silu(0)
            round_w13(0)
            with act.Fori(1, G) as i:
                g = act.snap(i)
                shared_silu(g)
                round_w13(g)
            sent_reg = act.alloc_register("sent")
            act.reg_mov(sent_reg, 0)

            def gate(n, u):
                at, q = slot(u, 0), u % 2
                act.wait_ge(up_done[at], turns(n, u, 0))
                after(act, hm_done[slot(u, 2)], turns(n, u, 2))
                A(hs[q][:], bank[2 + q][:, 0:HID], ACT.Silu).then_inc(silu_done[at], 1)

            def turned(n, u):
                at, q = slot(u, 1), (u - 1) % 2
                act.wait_ge(th_done[at], turns(n, u, 1))
                after(act, dn_done[slot(u, 3)], turns(n, u, 3))
                nc.scalar.copy(hmT[q][:], bank[4 + q][:, 0:HID]).then_inc(hmT_done[at], 1)

            def result(n, u):
                at, q, buf = slot(u, 2), u % 2, (u - 2) % U
                act.wait_ge(dn_done[at], turns(n, u, 2))
                if isinstance(n, int):
                    after(act, y_sent[buf], 16 * (n - 1 if u < 2 else n))
                else:
                    if buf == 0:
                        act.reg_add(sent_reg, sent_reg, 16)
                    act.wait_ge(y_sent[buf], sent_reg)
                nc.scalar.copy(ys[buf][:], bank[6 + q][:, 0:D]).then_inc(ys_done[at], 1)

            def act_step(n, u):
                if exists(n, u, 0):
                    gate(n, u)
                if exists(n, u, 1):
                    turned(n, u)
                if exists(n, u, 2):
                    result(n, u)

            expert_steps(act, act_step, 2)

            for j in range(J):
                rows = P if j < J - 1 else LAST
                act.wait_ge(res_tr, j + 1)
                nc.scalar.copy(res[0:rows, j, :], bank[j % 4][0:rows, 0:D]).then_inc(res_copied, 1)

            act.wait_ge(weight_done, 1)
            for j in range(J):
                rows = P if j < J - 1 else LAST
                if j % YC == 0:
                    act.wait_ge(y_loaded[1][j // YC], 16 * (2 if j // YC == J // YC - 1 else 1))
                A(result_rows[0:rows, 1, j, :], result_rows[0:rows, 1, j, :], ACT.Copy,
                  scale=weight[0:rows, 1, j:j + 1]).then_inc(scaled, 1)

        @block.gpsimd
        def _(pool):
            pool.wait_ge(s_cst, 16)
            pool.wait_ge(s_small, 160)
            nc.gpsimd.memset(pad[:], 0.0).then_inc(pad_ready, 1)
            pool.wait_ge(pad_ready, 1)
            nc.gpsimd.tensor_copy(pad[:, D:D + 1].bitcast(I32), dest_sb[:, 2 * J:2 * J + 1]).then_inc(pad_ready, 1)
            nc.gpsimd.tensor_copy(xd[:, :, :, D:D + 1].bitcast(I32),
                                  dest_sb[:, 0:2 * J].rearrange("p (j k o) -> p j k o", k=2, o=1)
                                  ).then_inc(ids_ready, 1)

            def group(p, n):
                g = 2 * n + p
                for k in range(4):
                    rows, half = PIECES[k][1], PIECES[k][2]
                    pool.wait_ge(ft_done[k], g + 1)
                    after(pool, rr_done[k], g)
                    sin = cst[0:rows, C_SIN + HD * half:C_SIN + HD * half + HD]
                    nc.gpsimd.tensor_tensor(
                        ss[k][0:rows, :].rearrange("p (h t e) -> p h t e", t=2, e=8),
                        ft[k][0:rows, :].rearrange("p (h t e) -> p h t e", t=2, e=8)[:, :, ::-1, :],
                        sin.rearrange("p (h t e) -> p h t e", h=1, t=2).broadcast_to([rows, 2 * H, 2, HD // 2]),
                        ALU.mult).then_inc(ss_done[k], 1)
                    if k == 0:
                        pool.wait_ge(lc_done, g + 1)
                        nc.gpsimd.tensor_tensor(hl[p][:], hl[p][:], hT[p][:], ALU.add).then_inc(lh_done, 1)

            two(pool, group)

            for j in range(J):
                rows = P if j < J - 1 else LAST
                pool.wait_ge(xd_ready, j // BATCH + 1 if j < JA else JA // BATCH + j - JA + 1)
                if j in (0, JA):
                    pool.wait_ge(pos_done, 1 if j == 0 else 2)
                if j == 0:
                    pool.wait_ge(ids_ready, 1)
                for k in range(2):
                    nc.gpsimd.indirect_dma_start(
                        out=xs_dram[:, :], out_offset=bass.IndirectOffsetOnAxis(ap=pos_i[0:rows, k, j:j + 1], axis=0),
                        in_=xd[0:rows, j, k, :], in_offset=None).then_inc(scattered, 16)

            bound_reg = pool.alloc_register("bound")
            pool.reg_mov(bound_reg, 2 * NTOK - 1)
            bound = pool.snap(bound_reg)
            count = [pool.alloc_register(f"count{i}") for i in range(SLOTS)]
            for c in count:
                pool.reg_mov(c, 1)

            with pool.Fori(0, TILES // U):
                for u in range(U):
                    pool.wait_ge(ys_done[u % SLOTS], count[u % SLOTS])
                    pool.reg_add(count[u % SLOTS], count[u % SLOTS], 1)
                    nc.gpsimd.indirect_dma_start(
                        out=y_dram[:, :],
                        out_offset=bass.IndirectOffsetOnAxis(ap=goal[u][:, 0:1].bitcast(I32), axis=0),
                        in_=ys[u][:], in_offset=None, bounds_check=bound, oob_is_err=False).then_inc(y_sent[u], 16)

            for c in range(ON_DVE, J // YC):
                pool.wait_ge(res_copied, (c + 1) * YC)
                pool.wait_ge(scaled, (c + 1) * YC)
                for rows, a, b in chunk_parts(c):
                    last = nc.gpsimd.tensor_tensor(result_rows[0:rows, 1, a:b, :], result_rows[0:rows, 1, a:b, :],
                                                   res[0:rows, a:b, :], ALU.add)
                last.then_inc(fin_p, 1)

        @block.vector
        def _(dve):
            V = nc.vector

            def patch(p, n):
                g = 2 * n + p
                dve.wait_ge(tok_done, g + 1)
                after(dve, lh_done, g - 1)
                V.scalar_tensor_tensor(
                    out=hT[p][:, :, 1:1 + NP_], in0=ps_tok[:, 0:P].rearrange("p (b t) -> p b t", b=2),
                    scalar=cols[:, 0:1],
                    in1=pos_sb[:, 1:1 + NP_].rearrange("p (o t) -> p o t", o=1).broadcast_to([P, 2, NP_]),
                    op0=ALU.add, op1=ALU.mult).then_inc(hpatch_done, 1)

            def norm1(p, n):
                g = 2 * n + p
                dve.wait_ge(rs1_done, g + 1)
                after(dve, qkv_done[3], g - 1)
                V.tensor_tensor(xT[p][:].rearrange("p b t -> p (b t)"), ps_dev1[:, 0:GN], rs1[:], ALU.mult).then_inc(xT_done, 1)

            def norm2(p, n):
                g = 2 * n + p
                dve.wait_ge(rs2_done, g + 1)
                V.tensor_tensor(x2T[:, bass.ds(g * GN, GN)], ps_dev2[:, 0:GN], rs2[:], ALU.mult).then_inc(x2_done, 1)

            def bias(g, k):
                n = PIECES[k][1]
                dve.wait_ge(qkv_done[k], g + 1)
                V.tensor_tensor(qk[k][0:n, :], ps_qkv[k % 2][0:n, 0:2 * D], bqk_sb[0:n, :], ALU.add
                                ).then_inc(qk_done[k], 1)

            def elu(g, k):
                n = PIECES[k][1]
                dve.wait_ge(ex_done[k], g + 1)
                after(dve, kv_done[k // 2], g)
                after(dve, ss_done[k], g)
                V.scalar_tensor_tensor(out=ft[k][0:n, :], in0=ex[k][0:n, :], scalar=1.0, in1=qk[k][0:n, :],
                                       op0=ALU.min, op1=ALU.max).then_inc(ft_done[k], 1)

            def cosine(g, k):
                n, half = PIECES[k][1], PIECES[k][2]
                dve.wait_ge(ft_done[k], g + 1)
                cos = cst[0:n, C_COS + HD * half:C_COS + HD * half + HD]
                V.tensor_tensor(cc[k][0:n, :].rearrange("p (h d) -> p h d", d=HD),
                                ft[k][0:n, :].rearrange("p (h d) -> p h d", d=HD),
                                cos.rearrange("p (h d) -> p h d", h=1).broadcast_to([n, 2 * H, HD]), ALU.mult).then_inc(cc_done[k], 1)

            def rotated(g, k):
                n = PIECES[k][1]
                dve.wait_ge(cc_done[k], g + 1)
                dve.wait_ge(ss_done[k], g + 1)
                V.tensor_tensor(rr[k][0:n, :], cc[k][0:n, :], ss[k][0:n, :], ALU.add).then_inc(rr_done[k], 1)

            def heads(g, j):
                dve.wait_ge(kv_done[j], g + 1)
                V.tensor_tensor(kvm[j][:, 0, :], ps_kv[:, 0:D], mask, ALU.mult)
                V.tensor_scalar(kvm[j][:, 1, :], mask, ps_kv[:, D:D + 1], None, ALU.mult).then_inc(kvm_done[j], 1)

            def attended(g, j):
                dve.wait_ge(zr_done[j], g + 1)
                V.tensor_tensor(ot[:, j, :], ps_od[:, 0:SEQ], zr[j][:], ALU.mult).then_inc(ot_done[j], 1)

            def taps(p, n):
                g = 2 * n + p
                dve.wait_ge(lh_done, g + 1)
                V.scalar_tensor_tensor(out=hl[p][:, :, 1:SEQ], in0=xT[p][:, :, 0:SEQ - 1], scalar=cols[:, 3:4],
                                       in1=hl[p][:, :, 1:SEQ], op0=ALU.mult, op1=ALU.add).then_inc(tap_done, 1)
                dve.wait_ge(tap_done, g + 1)
                V.scalar_tensor_tensor(out=hl[p][:, :, 0:SEQ - 1], in0=xT[p][:, :, 1:SEQ], scalar=cols[:, 5:6],
                                       in1=hl[p][:, :, 0:SEQ - 1], op0=ALU.mult, op1=ALU.add).then_inc(hl_done, 1)

            def add(p, n):
                g = 2 * n + p
                dve.wait_ge(hl_done, g + 1)
                dve.wait_ge(ot_done[0], g + 1)
                dve.wait_ge(ot_done[1], g + 1)
                V.tensor_tensor(h2T[:, bass.ds(g * GN, GN)].rearrange("p (b t) -> p b t", b=2), ot[:], hl[p][:],
                                ALU.add).then_inc(h2_done, 1)

            steps = [0]
            chain = route_chain

            def then(ins):
                steps[0] += 1
                ins.then_inc(chain, 1)
                dve.wait_ge(chain, steps[0])

            def per_tile(ap):
                return ap.rearrange("p (j o) -> p j o", o=1).broadcast_to([P, ap.shape[1], E])

            def per_expert(ap, n):
                return ap.rearrange("p (o e) -> p o e", o=1).broadcast_to([P, n, E])

            def scores_of(ps, a, b):
                return ps[:, a * E:b * E].rearrange("p (j e) -> p j e", e=E)

            def first_best(a, b, scores, best, one_hot):
                then(V.tensor_reduce(best, scores, AX.X, ALU.max))
                then(V.tensor_tensor(eq[:, a:b], scores, per_tile(best), ALU.is_equal))
                then(V.tensor_tensor(wk[:, a:b], eq[:, a:b], per_expert(cst[:, C_RANK:C_RANK + E], b - a), ALU.mult))
                then(V.tensor_reduce(rk[:, a:b], wk[:, a:b], AX.X, ALU.max))
                then(V.tensor_tensor(one_hot, wk[:, a:b], per_tile(rk[:, a:b]), ALU.is_equal))

            def without(scores, one_hot):
                then(V.scalar_tensor_tensor(out=scores, in0=one_hot, scalar=-1e30, in1=scores,
                                            op0=ALU.mult, op1=ALU.add))

            def first_choices(a, b):
                first_best(a, b, scb[:, a:b], mx[:, a:b], pick[:, 0, a:b])

            def second_choices(a, b):
                without(scb[:, a:b], pick[:, 0, a:b])
                first_best(a, b, scb[:, a:b], mx[:, a:b], pick[:, 1, a:b])
                V.tensor_tensor(both[:, a:b], pick[:, 0, a:b], pick[:, 1, a:b], ALU.add).then_inc(both_ready, 1)

            def places(a, b, before, total):
                i, n = (0, b - a) if a == 0 else (1, b - a)
                then(V.tensor_copy(cnt[i][:], total.rearrange("p (j e) -> p e j", e=E)))
                last = V.tensor_tensor(place[:, a:b], before.rearrange("p (j e) -> p j e", e=E),
                                       per_expert(cst[:, C_BASE:C_BASE + E], n), ALU.add)
                counts = cnt[i]
                if a == 0:
                    last.then_inc(ahead_read, 1)
                else:
                    V.tensor_copy(cnt_on[:, :, 1:n], cnt[1][:, :, 1:n])
                    then(V.tensor_tensor(cnt_on[:, :, 0], cnt[1][:, :, 0], inc[0][:, :, JA - 1], ALU.add))
                    counts = cnt_on
                then(V.tensor_tensor_scan(inc[i][:].rearrange("p e j -> p (e j)"),
                                          cst[:, C_RESET + E * a:C_RESET + E * b],
                                          counts[:].rearrange("p e j -> p (e j)"), 0.0, ALU.mult, ALU.add))
                then(V.tensor_tensor(exc[i][:], inc[i][:], cnt[i][:], ALU.subtract))
                then(V.tensor_tensor(place[:, a:b], place[:, a:b], exc[i][:].rearrange("p e j -> p j e"), ALU.add))
                then(V.tensor_tensor(prod[:, :, a:b], pick[:, :, a:b],
                                     place[:, a:b].rearrange("p (o j) e -> p o j e", o=1)
                                     .broadcast_to([P, 2, n, E]), ALU.mult))
                then(V.tensor_reduce(pos_f[:, :, a:b], prod[:, :, a:b], AX.X, ALU.add))
                V.tensor_copy(pos_i[:, :, a:b], pos_f[:, :, a:b]).then_inc(pos_done, 1)

            def choices_ahead():
                dve.wait_ge(gate_done, (G - 2) * GN // P)
                then(V.tensor_tensor(scb[:, 0:JA], scores_of(ps_gate, 0, JA), per_expert(gateb_sb[:], JA), ALU.add))
                V.tensor_copy(sc[:, 0:JA], scores_of(ps_gate, 0, JA)).then_inc(ahead_read, 1)
                first_choices(0, JA)

            def places_ahead():
                dve.wait_ge(pref_done, 1)
                places(0, JA, ps_ahead[:, 0:JA * E], ps_ahead[:, JA * E:2 * JA * E])

            def group(p, n, first=False, last=False):
                g = 2 * n + p
                before = (1 - p, n - 1 if p == 0 else n)
                behind = (1 - p, n if p == 0 else n + 1)
                bias(g, 0)
                bias(g, 1)
                if not first:
                    heads(g - 1, 1)
                elu(g, 0)
                cosine(g, 0)
                elu(g, 1)
                cosine(g, 1)
                rotated(g, 0)
                rotated(g, 1)
                if not first:
                    attended(g - 1, 1)
                    add(*before)
                bias(g, 2)
                if not last:
                    patch(*behind)
                bias(g, 3)
                elu(g, 2)
                cosine(g, 2)
                elu(g, 3)
                cosine(g, 3)
                heads(g, 0)
                taps(p, n)
                rotated(g, 2)
                rotated(g, 3)
                if not last:
                    norm1(*behind)
                else:
                    choices_ahead()
                attended(g, 0)
                if not first:
                    norm2(*before)

            dve.wait_ge(s_small, 160)
            dve.wait_ge(s_cst, 16)
            for i in range(2):
                V.tensor_tensor(hT[i][:, :, 0], cols[:, 1:2].broadcast_to([P, 2]),
                                pos_sb[:, 0:1].broadcast_to([P, 2]), ALU.mult).then_inc(cls_ready, 1)
            V.memset(scb[:], 0.0)
            V.memset(sc[:], 0.0).then_inc(cls_ready, 1)
            V.tensor_scalar(bqk_sb[:], bqk_sb[:], 1.0, None, ALU.add).then_inc(cls_ready, 1)
            dve.wait_ge(cls_ready, 4)
            patch(0, 0)
            norm1(0, 0)
            group(0, 0, first=True)
            with dve.Fori(0, G // 2 - 1) as i:
                n = dve.snap(i)
                group(1, n)
                group(0, n + 1)
            group(1, G // 2 - 1, last=True)
            heads(G - 1, 1)
            second_choices(0, JA)
            attended(G - 1, 1)
            add(1, G // 2 - 1)
            places_ahead()
            norm2(1, G // 2 - 1)

            dve.wait_ge(gate_done, J)
            dve.wait_ge(cls_ready, 3)
            V.tensor_tensor(scb[0:LAST, J - 1, :], ps_gate[0:LAST, (J - 1) * E:J * E], gateb_sb[0:LAST, :], ALU.add)
            then(V.tensor_tensor(scb[:, JA:J - 1, :], scores_of(ps_gate, JA, J - 1),
                                 per_expert(gateb_sb[:], J - 1 - JA), ALU.add))
            first_choices(JA, J)
            second_choices(JA, J)
            V.tensor_copy(sc[:, JA:J - 1, :], scores_of(ps_gate, JA, J - 1))
            V.tensor_copy(sc[0:LAST, J - 1, :], ps_gate[0:LAST, (J - 1) * E:J * E])
            dve.wait_ge(pref_done, 2)
            places(JA, J, ps_before[:, 0:(J - JA) * E], ps_total[:, 0:(J - JA) * E])
            first_best(0, J, sc[:], top[:, 0, :], pick_u[:])
            without(sc[:], pick_u[:])
            V.tensor_reduce(top[:, 1, :], sc[:], AX.X, ALU.max).then_inc(route, 1)
            def shared_mul(g):
                for m in range(2):
                    dve.wait_ge(sh_act, 2 * g + m + 1)
                    if m == 0:
                        after(dve, sh_down, g)
                    V.tensor_tensor(sh_h[m][:], sh_s[m][:], bank[2 + m][:, 0:GN], ALU.mult).then_inc(sh_mul, 1)
                dve.wait_ge(sh_down, g + 1)
                V.tensor_tensor(h2T[:, bass.ds(g * GN, GN)], h2T[:, bass.ds(g * GN, GN)], bank[4][:, 0:GN], ALU.add
                                ).then_inc(sh_add, 1)

            def remainder_w13(e):
                dve.wait_ge(wh_done, e + 1)
                part = bass.ds(e * 2 * HID, 2 * HID)
                V.tensor_tensor(w13_l[:, part], w13_flat[:, part], w13_h[:, part], ALU.subtract).then_inc(wl_done, 1)

            shared_mul(0)
            remainder_w13(0)
            n_e = inc[1][:, :, J - JA - 1]
            then(V.tensor_scalar(tn[:], n_e, float(P - 1), None, ALU.add))
            then(V.tensor_copy(ti[:, 0, :], tn[:]))
            then(V.tensor_scalar(ti[:, 1, :], ti[:, 0, :], 7, None, ALU.arith_shift_right))
            then(V.tensor_copy(tf[:], ti[:, 1, :]))
            then(V.tensor_tensor_scan(te[:], cst[:, C_ONE:C_ONE + E], tf[:], 0.0, ALU.mult, ALU.add))
            def tiles_of(ap):
                return ap.rearrange("p (o e) -> p o e", o=1).broadcast_to([P, TILES, E])
            iota = cst[:, C_IOTA:C_IOTA + TILES]
            then(V.tensor_tensor(ge[:], iota.rearrange("p (t o) -> p t o", o=1).broadcast_to([P, TILES, E]),
                                 tiles_of(te[:]), ALU.is_ge))
            then(V.tensor_reduce(t_e[:], ge[:], AX.X, ALU.add))
            shared_mul(1)
            remainder_w13(1)
            then(V.tensor_tensor(gn[:], ge[:], tiles_of(tf[:]), ALU.mult))
            then(V.tensor_reduce(t_s[:], gn[:], AX.X, ALU.add))
            then(V.tensor_tensor(t_s[:], iota, t_s[:], ALU.subtract))
            then(V.tensor_scalar(t_r[:, 0, :], t_e[:], float(CAP), None, ALU.mult))
            then(V.scalar_tensor_tensor(out=t_r[:, 1, :], in0=t_s[:], scalar=float(P), in1=t_r[:, 0, :],
                                        op0=ALU.mult, op1=ALU.add))
            then(V.tensor_scalar(t_r[:, 1, :], t_r[:, 1, :], float(E * CAP), None, ALU.min))
            then(V.tensor_copy(tab_r[:], t_r[:, 1, :]))
            then(V.tensor_scalar(t_e[:], t_e[:], float(E - 1), float(2 * D), ALU.min, ALU.mult))
            then(V.tensor_copy(tab_e[:], t_e[:]))
            then(V.tensor_tensor(tn[:], n_e, cst[:, C_BASE:C_BASE + E], ALU.add))
            V.tensor_copy(tab_p[:], tn[:]).then_inc(tab_done, 1)
            shared_mul(2)
            remainder_w13(2)
            dve.wait_ge(sg_e, 1)
            then(V.tensor_scalar(sg[:], sg[:], 1.0, None, ALU.add))
            then(V.reciprocal(sg[:], sg[:]))
            then(V.tensor_tensor(mx[:], sg[:, 0, :], sg[:, 1, :], ALU.add))
            then(V.reciprocal(mx[:], mx[:]))
            for k in range(2):
                last = V.tensor_tensor(weight[:, k, :], sg[:, k, :], mx[:], ALU.mult)
            last.then_inc(weight_done, 1)
            with dve.Fori(3, G) as i:
                g = dve.snap(i)
                shared_mul(g)
                remainder_w13(g)

            sent_reg = dve.alloc_register("sent")
            dve.reg_mov(sent_reg, 0)
            seen_xh = dve.alloc_register("seen_xh")
            dve.reg_mov(seen_xh, 0)

            def untransposed(n, u):
                q = u % 2
                dve.wait_ge(tx_done[slot(u, 0)], turns(n, u, 0))
                after(dve, up_done[slot(u, 2)], turns(n, u, 2))
                V.tensor_copy(xsT_h[q][:], bank[q][:, 0:P]).then_inc(xh_done, 1)
                dve.reg_add(seen_xh, seen_xh, 1)
                dve.wait_ge(xh_done, seen_xh)
                V.tensor_tensor(xsT_l[q][:], bank[q][:, 0:P], xsT_h[q][:], ALU.subtract
                                ).then_inc(xsT_done[slot(u, 0)], 1)

            def gated(n, u):
                at, q, buf = slot(u, 2), u % 2, (u - 2) % U
                if isinstance(n, int):
                    after(dve, y_sent[buf], 16 * (n - 1 if u < 2 else n))
                else:
                    if buf == 0:
                        dve.reg_add(sent_reg, sent_reg, 16)
                    dve.wait_ge(y_sent[buf], sent_reg)
                V.tensor_copy(goal[buf][:], xs[buf][:, D:ROW])
                dve.wait_ge(silu_done[at], turns(n, u, 2))
                after(dve, th_done[slot(u, 4)], turns(n, u, 4))
                V.tensor_tensor(hm[q][:], hs[q][:], bank[2 + q][:, HID:2 * HID], ALU.mult).then_inc(hm_done[at], 1)

            def dve_step(n, u):
                if exists(n, u, 0):
                    untransposed(n, u)
                if exists(n, u, 2):
                    gated(n, u)

            expert_steps(dve, dve_step, 2)

            for c in range(ON_DVE):
                dve.wait_ge(res_copied, (c + 1) * YC)
                dve.wait_ge(scaled, (c + 1) * YC)
                for rows, a, b in chunk_parts(c):
                    last = V.tensor_tensor(result_rows[0:rows, 1, a:b, :], result_rows[0:rows, 1, a:b, :],
                                           res[0:rows, a:b, :], ALU.add)
                last.then_inc(fin_v, 1)
            for c in range(J // YC):
                if c < ON_DVE:
                    dve.wait_ge(fin_v, c + 1)
                else:
                    dve.wait_ge(fin_p, c + 1 - ON_DVE)
                dve.wait_ge(y_loaded[0][c], 16 * len(chunk_parts(c)))
                for j in range(c * YC, (c + 1) * YC):
                    rows = P if j < J - 1 else LAST
                    last = V.scalar_tensor_tensor(
                        out=result_rows[0:rows, 0, j, :], in0=result_rows[0:rows, 0, j, :],
                        scalar=weight[0:rows, 0, j:j + 1], in1=result_rows[0:rows, 1, j, :],
                        op0=ALU.mult, op1=ALU.add)
                last.then_inc(fin_done, 1)

        @block.tensor
        def _(pe):
            M, T = nc.tensor.matmul, nc.tensor.transpose

            def tokens(p, n, part, first=False):
                g = 2 * n + p
                if part == 0:
                    after(pe, x_loaded[p], 32 * n + 32 * p)
                    after(pe, xT_done, g)
                for k in range(*((0, KB // 2), (KB // 2, KB))[part]):
                    if first and k in FIRST_AT:
                        pe.wait_ge(first_loaded[FIRST_AT[k]], 32)
                    M(ps_tok[:, 0:P], wt[:, k, :], xp[p][:, k, :], start=(k == 0), stop=False)
                if part == 1:
                    if first:
                        pe.wait_ge(s_wtok, 32)
                    M(ps_tok[:, 0:P], wt_rest[:], xr[p][:], start=False, stop=True).then_inc(tok_done, 1)

            def centre_1(p, n):
                g = 2 * n + p
                pe.wait_ge(hpatch_done, g + 1)
                pe.wait_ge(txt_loaded[p], 16 * n + 16)
                M(ps_dev1[:, 0:GN], center_w, hT[p][:].rearrange("p b t -> p (b t)"), start=True, stop=True
                  ).then_inc(dev1_done, 1)

            def var_1(p, n):
                g = 2 * n + p
                pe.wait_ge(sq1_done, g + 1)
                M(ps_var[:, 0:GN], mean_w, sq1[:], start=True, stop=True).then_inc(var1, 1)

            def centre_2(p, n):
                g = 2 * n + p
                pe.wait_ge(h2_done, g + 1)
                M(ps_dev2[:, 0:GN], center_w, h2T[:, bass.ds(g * GN, GN)], start=True, stop=True
                  ).then_inc(dev2_done, 1)

            def var_2(p, n, behind_1=True):
                g = 2 * n + p
                pe.wait_ge(sq2_done, g + 1)
                if behind_1:
                    pe.wait_ge(lv1_done, g + 3)
                M(ps_var[:, 0:GN], mean_w, sq2[:], start=True, stop=True).then_inc(var2, 1)

            def project(p, g, k):
                at, rows, _ = PIECES[k]
                x = xT[p][:].rearrange("p b t -> p (b t)")[:, at:at + rows]
                if k == 0:
                    pe.wait_ge(xT_done, g + 1)
                if k < 2:
                    after(pe, qk_done[k + 2], g)
                    after(pe, v_done[k + 2], g)
                else:
                    pe.wait_ge(qk_done[k - 2], g + 1)
                    pe.wait_ge(v_done[k - 2], g + 1)
                M(ps_qkv[k % 2][0:rows, 0:2 * D], x, wqk_sb[:], start=True, stop=True)
                T(ps_qkv[k % 2][0:rows, 2 * D:3 * D], x, ident).then_inc(qkv_done[k], 1)

            def turn(g, j):
                after(pe, qq_done[1 - j], g + j)
                for k in (2 * j, 2 * j + 1):
                    at, rows = PIECES[k][0] - j * SEQ, PIECES[k][1]
                    pe.wait_ge(ft_done[k], g + 1)
                    T(ps_tr[:, at:at + rows], ft[k][0:rows, 0:D], ident[0:rows, 0:rows])
                    pe.wait_ge(rr_done[k], g + 1)
                    last = T(ps_tr[:, SEQ + at:SEQ + at + rows], rr[k][0:rows, 0:D], ident[0:rows, 0:rows])
                last.then_inc(qT_done[j], 1)

            def sums(g, j):
                after(pe, kvm_done[1 - j], g + j)
                for i, k in enumerate((2 * j, 2 * j + 1)):
                    rows = PIECES[k][1]
                    pe.wait_ge(v_done[k], g + 1)
                    M(ps_kv[:, 0:D], rr[k][0:rows, D:2 * D], vt[k][0:rows, :], start=(i == 0), stop=(i == 1))
                for i, k in enumerate((2 * j, 2 * j + 1)):
                    rows = PIECES[k][1]
                    last = M(ps_kv[:, D:D + 2], ft[k][0:rows, D:2 * D], ones[0:rows, 0:2], start=(i == 0), stop=(i == 1))
                last.then_inc(kv_done[j], 1)

            def attend(g, j):
                pe.wait_ge(kvm_done[j], g + 1)
                pe.wait_ge(qq_done[j], g + 1)
                after(pe, ot_done[1 - j], g + j)
                M(ps_od[:, 0:SEQ], kvm[j][:, 0, :], qq[j][:, 1, :], start=True, stop=True)
                M(ps_od[:, SEQ:2 * SEQ], kvm[j][:, 1, :], qq[j][:, 0, :], start=True, stop=True
                  ).then_inc(od_done[j], 1)

            gate_most, gate_rest = (G - 2) * GN // P, (G - 1) * GN // P

            def rows_ahead(i):
                if i == 0:
                    pe.wait_ge(qk_done[3], G)
                    pe.wait_ge(v_done[3], G)
                after(pe, xd_ready, i)
                for j in range(BATCH):
                    at = P * (BATCH * i + j)
                    last = T(ps_rows[:, P * j:P * j + P], x2T[:, at:at + P], ident)
                last.then_inc(xd_tr, 1)

            def counts(a, b, before, total):
                flat = both[:].rearrange("p j e -> p (j e)")
                full = (min(b, J - 1) - a) * E
                for ps, w in ((before, tri), (total, ones)):
                    last = M(ps[:, 0:full], w, flat[:, a * E:a * E + full], start=True, stop=True)
                    if b == J:
                        last = M(ps[:, full:full + E], w[0:LAST, :], flat[0:LAST, (J - 1) * E:J * E],
                                 start=True, stop=True)
                last.then_inc(pref_done, 1)

            def gate(first, end):
                for j in range(first, end):
                    rows = P if j < J - 1 else LAST
                    M(ps_gate[0:rows, E * j:E * j + E], x2T[:, P * j:P * j + rows], gate_sb[:],
                      start=True, stop=True).then_inc(gate_done, 1)

            def group(p, n, first=False, last=False):
                g = 2 * n + p
                before = (1 - p, n - 1 if p == 0 else n)
                behind = (1 - p, n if p == 0 else n + 1)
                project(p, g, 0)
                project(p, g, 1)
                if not first:
                    turn(g - 1, 1)
                    sums(g - 1, 1)
                if not last:
                    tokens(*behind, 0)
                else:
                    pe.wait_ge(x2_done, G - 2)
                    gate(0, JA)
                if not first:
                    attend(g - 1, 1)
                project(p, g, 2)
                if not last:
                    tokens(*behind, 1)
                else:
                    gate(JA, gate_most)
                project(p, g, 3)
                if not first:
                    centre_2(*before)
                if not last:
                    centre_1(*behind)
                turn(g, 0)
                sums(g, 0)
                if not last:
                    var_1(*behind)
                attend(g, 0)
                if not first:
                    var_2(*before, behind_1=not last)

            tokens(0, 0, 0, first=True)
            tokens(0, 0, 1, first=True)
            pe.wait_ge(s_cst, 16)
            pe.wait_ge(s_small, 160)
            pe.wait_ge(cls_ready, 4)
            centre_1(0, 0)
            var_1(0, 0)
            group(0, 0, first=True)
            with pe.Fori(0, G // 2 - 1) as i:
                n = pe.snap(i)
                group(1, n)
                group(0, n + 1)
            group(1, G // 2 - 1, last=True)
            turn(G - 1, 1)
            sums(G - 1, 1)
            attend(G - 1, 1)
            rows_ahead(0)
            centre_2(1, G // 2 - 1)
            pe.wait_ge(x2_done, G - 1)
            pe.wait_ge(ahead_read, 1)
            gate(gate_most, gate_rest)
            pe.wait_ge(both_ready, 1)
            pe.wait_ge(qk_done[2], G)
            pe.wait_ge(v_done[2], G)
            counts(0, JA, ps_ahead[:, 0:JA * E], ps_ahead[:, JA * E:2 * JA * E])
            var_2(1, G // 2 - 1, behind_1=False)
            for i in range(1, JA // BATCH):
                rows_ahead(i)

            pe.wait_ge(x2_done, G)
            gate(gate_rest, J)

            def turn_row(j):
                rows = P if j < J - 1 else LAST
                if j >= JA + 2:
                    pe.wait_ge(xd_ready, JA // BATCH + j - JA - 1)
                T(bank[5 + j % 2][0:rows, 0:D], x2T[:, P * j:P * j + rows], ident).then_inc(xd_tr, 1)

            for j in range(JA, (JA + J) // 2):
                turn_row(j)
            pe.wait_ge(both_ready, 2)
            counts(JA, J, ps_before[:, 0:(J - JA) * E], ps_total[:, 0:(J - JA) * E])
            for j in range((JA + J) // 2, J):
                turn_row(j)

            pe.wait_ge(s_wexp, 96)
            pe.wait_ge(pos_done, 2)
            def shared(g):
                x = x2T[:, bass.ds(g * GN, GN)]
                after(pe, sh_mul, 2 * g)
                for m in range(2):
                    M(bank[2 + m][:, 0:GN], sw13[:, HID + P * m:HID + P * m + P], x, start=True, stop=True)
                    M(bank[m][:, 0:GN], sw13[:, P * m:P * m + P], x, start=True, stop=True).then_inc(sh_up, 1)
                after(pe, sh_add, g)
                for m in range(2):
                    pe.wait_ge(sh_mul, 2 * g + m + 1)
                    last = M(bank[4][:, 0:GN], sw2_sb[:, m, :], sh_h[m][:], start=(m == 0), stop=(m == 1))
                last.then_inc(sh_down, 1)

            shared(0)
            with pe.Fori(1, G) as i:
                shared(pe.snap(i))
            pe.wait_ge(sh_add, G)

            pe.wait_ge(tab_done, 1)

            at_w2 = {}
            carried = {u: pe.alloc_register(f"at_w2_{u}") for u in range(U - 4, U)}

            def expert_at(u, back):
                if u >= back:
                    return at_w2[u - back]
                return pe.snap(carried[u - back + U], min_val=0, max_val=(E - 1) * 2 * D)

            tile_no = pe.alloc_register("tile_no")
            pe.reg_mov(tile_no, 0)

            def transposed(n, u):
                q = u % 2
                t = pe.snap(tile_no, min_val=0, max_val=TILES - 1) if not isinstance(n, int) else U * n + u
                loaded_at = pe.alloc_register(f"at_w2_{u}_{'in_loop' if not isinstance(n, int) else 'first'}")
                pe.reg_load(loaded_at, tab_e[0:1, bass.ds(t, 1)])
                pe.reg_add(tile_no, tile_no, 1)
                if u in carried:
                    pe.reg_mov(carried[u], loaded_at)
                at_w2[u] = pe.snap(loaded_at, donate=True, min_val=0, max_val=(E - 1) * 2 * D)
                pe.wait_ge(xs_loaded[u], 16 * n + 16 if isinstance(n, int) else loaded)
                T(bank[q][:, 0:P], xs[u][:, 0:D], ident).then_inc(tx_done[slot(u, 0)], 1)

            def up(n, u):
                at, q = slot(u, 2), u % 2
                first = expert_at(u, 2)
                pe.wait_ge(xsT_done[at], turns(n, u, 2))
                terms = [(xsT_h, w13_h), (xsT_h, w13_l), (xsT_l, w13_h)]
                for i, (x, w) in enumerate(terms):
                    last = M(bank[2 + q][:, 0:2 * HID], x[q][:], w[:, bass.ds(first * 2, 2 * HID)],
                             start=(i == 0), stop=(i == 2))
                last.then_inc(up_done[at], 1)

            def hidden(n, u):
                at, q = slot(u, 3), (u - 1) % 2
                pe.wait_ge(hm_done[at], turns(n, u, 3))
                for m in range(2):
                    last = T(bank[4 + q][:, P * m:P * m + P], hm[q][:, P * m:P * m + P], ident)
                last.then_inc(th_done[at], 1)

            def down(n, u):
                at, q = slot(u, 4), u % 2
                w = w2_sb[:].rearrange("p e k d -> p (e k d)")
                first = expert_at(u, 4)
                pe.wait_ge(hmT_done[at], turns(n, u, 4))
                after(pe, ys_done[slot(u, 6)], turns(n, u, 6))
                for m in range(2):
                    last = M(bank[6 + q][:, 0:D], hmT[q][:, m, :], w[:, bass.ds(first + m * D, D)],
                             start=(m == 0), stop=(m == 1))
                last.then_inc(dn_done[at], 1)

            loaded = pe.alloc_register("loaded")
            pe.reg_mov(loaded, 16)

            def pe_step(n, u):
                if exists(n, u, 2):
                    up(n, u)
                if u == 0 and not isinstance(n, int):
                    pe.reg_add(loaded, loaded, 16)
                if exists(n, u, 0):
                    transposed(n, u)
                if exists(n, u, 3):
                    hidden(n, u)
                if exists(n, u, 4):
                    down(n, u)

            pe.wait_ge(wl_done, E)
            expert_steps(pe, pe_step, 4)
            for j in range(J):
                rows = P if j < J - 1 else LAST
                after(pe, res_copied, j - 3)
                T(bank[j % 4][0:rows, 0:D], h2T[:, P * j:P * j + rows], ident).then_inc(res_tr, 1)


_OUT = (NTOK, D)


def kernel(x, txt, L0_tok_W, L0_tok_b, L0_tok_class_token, L0_tok_pos_embed, L0_attn_Wqk, L0_attn_bqk,
           L0_attn_lepe_w, L0_attn_lepe_b, L0_ffn_gate_w, L0_ffn_biases, L0_ffn_w1, L0_ffn_w3, L0_ffn_w2,
           L0_ffn_sw1, L0_ffn_sw3, L0_ffn_sw2):
    import concourse.bacc as bacc
    from concourse.bass_utils import run_bass_kernel_spmd

    con = np.ascontiguousarray
    patches = x.reshape(G, 2, CH, GRID, PATCH, GRID, PATCH).transpose(0, 2, 4, 6, 1, 3, 5)
    arrays = {
        "patches": con(patches).reshape(G * IN_D, 2 * NP_),
        "txt": con(txt.transpose(2, 0, 1)).reshape(D, B * NT),
        "w_tok": con(L0_tok_W.transpose(1, 0)),
        "b_tok": L0_tok_b.reshape(D, 1),
        "cls": L0_tok_class_token.reshape(D, 1),
        "pos": con(L0_tok_pos_embed.transpose(1, 0)),
        "wqk": con(L0_attn_Wqk),
        "bqk": L0_attn_bqk.reshape(1, 2 * D),
        "lepe_w": L0_attn_lepe_w.reshape(D, 3),
        "lepe_b": L0_attn_lepe_b.reshape(D, 1),
        "gate_w": con(L0_ffn_gate_w.transpose(1, 0)),
        "gate_b": L0_ffn_biases.reshape(1, E),
        "w1": con(L0_ffn_w1), "w3": con(L0_ffn_w3), "w2": con(L0_ffn_w2),
        "sw1": con(L0_ffn_sw1), "sw3": con(L0_ffn_sw3), "sw2": con(L0_ffn_sw2),
        "consts": constants(),
        "dests": destinations(),
    }
    arrays = {f"in_{k}": np.asarray(v) for k, v in arrays.items()}
    nc = bacc.Bacc("TRN2", target_bir_lowering=False, num_devices=1)
    args = [nc.dram_tensor(k, a.shape, mybir.dt.from_np(a.dtype), kind="ExternalInput").ap()
            for k, a in arrays.items()]
    args.append(nc.dram_tensor("out_tokens", _OUT, F32, kind="ExternalOutput").ap())
    build(nc, *args)
    r = run_bass_kernel_spmd(nc, [arrays], core_ids=[0])
    return np.asarray(r.results[0]["out_tokens"]).reshape(B, SEQ, D)
```
